# Optimizing a Trainium2 kernel written in Bass

```python
import numpy as np
import jax
import jax.numpy as jnp

def _softmax(x, axis=-1):
    return jax.nn.softmax(x, axis=axis)

def _gelu(x):
    return jax.nn.gelu(x, approximate=True)

def _silu(x):
    return jax.nn.silu(x)

def _sigmoid(x):
    return jax.nn.sigmoid(x)

def _layernorm(x, axis=-1, eps=1e-05):
    m = jnp.mean(x, axis=axis, keepdims=True)
    v = jnp.var(x, axis=axis, keepdims=True)
    return (x - m) / jnp.sqrt(v + eps)

def _scatter_add(tgt, idx, src, axis=0):
    return tgt.at[idx].add(src)

def _segment_sum(src, seg, n):
    return jax.ops.segment_sum(src, seg, n)
kernel_name = 'mk_decoder_postln_d2_seqx_r8_ccb777'

def setup_inputs(seed: int=0):
    np.random.seed(seed)
    _w = jnp.asarray

    def _rec_inputs():
        import jax
        import jax.numpy as jnp
        _rk = jax.random.key(seed)
        x = -0.000125 + 0.9999 * jax.random.normal(jax.random.fold_in(_rk, 1), (8, 128, 128), jnp.float32)
        _lenS = 128 - jax.random.randint(jax.random.fold_in(_rk, 7), (8,), 0, max(1, 128 // 4) + 1, jnp.int32)
        _lenS2 = 77 - jax.random.randint(jax.random.fold_in(_rk, 8), (8,), 0, max(1, 77 // 4) + 1, jnp.int32)
        _ctx_1024P = jax.random.normal(jax.random.fold_in(_rk, 11), (8, 16, 128), jnp.float32)
        _ctx_1024c = jax.random.dirichlet(jax.random.fold_in(_rk, 511), 0.3 * jnp.ones((16,), jnp.float32), (8, 77))
        _ctx_1024t = jnp.einsum('bsk,bkd->bsd', _ctx_1024c, _ctx_1024P)
        _ctx_1024t = _ctx_1024t * jax.lax.rsqrt(jnp.mean(jnp.square(_ctx_1024t)) + 1e-12) * 0.953939
        ctx_1024 = -0.000188977 + 0.999793 * (_ctx_1024t + 0.3 * jax.random.normal(jax.random.fold_in(_rk, 611), (8, 77, 128), jnp.float32))
        return (x, ctx_1024)
    x, ctx_1024 = _rec_inputs()

    def _L0_attn_setup():
        import jax, jax.numpy as jnp
        import numpy as np
        import math
        D_MODEL = 128
        N_HEADS = 16
        HEAD_DIM = D_MODEL // N_HEADS
        ROT_DIM = min(32, D_MODEL // 4)

        def _xavier(key, fan_in, fan_out):
            lim = math.sqrt(6.0 / (fan_in + fan_out))
            return jax.random.uniform(key, (fan_in, fan_out), jnp.float32, -lim, lim)
        key = jax.random.key(seed)
        ks = jax.random.split(key, 6)
        x = jax.random.normal(ks[0], (2, 256, D_MODEL), jnp.float32)
        Wq = _xavier(ks[1], D_MODEL, D_MODEL)
        Wk = _xavier(ks[2], D_MODEL, D_MODEL)
        Wv = _xavier(ks[3], D_MODEL, D_MODEL)
        Wr = _xavier(ks[4], D_MODEL, N_HEADS * ROT_DIM)
        Wo = _xavier(ks[5], D_MODEL, D_MODEL)
        z = jnp.zeros((D_MODEL,), jnp.float32)
        zr = jnp.zeros((N_HEADS * ROT_DIM,), jnp.float32)
        return {'x': x, 'Wq': Wq, 'bq': z, 'Wk': Wk, 'bk': z, 'Wv': Wv, 'bv': z, 'Wr': Wr, 'br': zr, 'Wo': Wo, 'bo': z}
    _L0_attn_all = _L0_attn_setup()
    _L0_attn_in = {k: v for k, v in _L0_attn_all.items() if k in ('Wq', 'bq', 'Wk', 'bk', 'Wv', 'bv', 'Wr', 'br', 'Wo', 'bo')}
    del _L0_attn_all

    def _L0_xattn_setup():
        import jax, jax.numpy as jnp
        import numpy as np
        HEADS = 16
        DIM_HEAD = 64
        INNER = HEADS * DIM_HEAD
        QUERY_DIM = 128
        CONTEXT_DIM = 128
        TEXT_LEN = 77
        IMG_SCALE = 1.0
        SCALE = DIM_HEAD ** (-0.5)

        def _attend(q, k, v):
            sim = jnp.einsum('bihd,bjhd->bhij', q, k) * SCALE
            attn = jax.nn.softmax(sim, axis=-1)
            out = jnp.einsum('bhij,bjhd->bihd', attn, v)
            B, N, H, D = out.shape
            return out.reshape(B, N, H * D)
        key = jax.random.key(seed)
        ks = jax.random.split(key, 10)
        B, N, Lc = (16, 256, 333)
        x = jax.random.normal(ks[0], (B, N, QUERY_DIM), dtype=jnp.float32)
        context = jax.random.normal(ks[1], (B, Lc, CONTEXT_DIM), dtype=jnp.float32)

        def w(k, din, dout):
            return jax.random.normal(k, (din, dout), dtype=jnp.float32) * din ** (-0.5)
        Wq = w(ks[2], QUERY_DIM, INNER)
        Wk = w(ks[3], CONTEXT_DIM, INNER)
        Wv = w(ks[4], CONTEXT_DIM, INNER)
        Wk_ip = w(ks[5], CONTEXT_DIM, INNER)
        Wv_ip = w(ks[6], CONTEXT_DIM, INNER)
        Wo = w(ks[7], INNER, QUERY_DIM)
        bo = jnp.zeros((QUERY_DIM,), dtype=jnp.float32)
        return {'x': x, 'context': context, 'Wq': Wq, 'Wk': Wk, 'Wv': Wv, 'Wk_ip': Wk_ip, 'Wv_ip': Wv_ip, 'Wo': Wo, 'bo': bo}
    _L0_xattn_all = _L0_xattn_setup()
    _L0_xattn_in = {k: v for k, v in _L0_xattn_all.items() if k in ('Wq', 'Wk', 'Wv', 'Wk_ip', 'Wv_ip', 'Wo', 'bo')}
    del _L0_xattn_all

    def _L0_ffn_setup():
        import jax, jax.numpy as jnp
        import numpy as np
        N_EXPERTS = 8
        CAP_FACTOR = 1.25
        BATCH, SEQ, DMODEL, DFF = (4, 256, 128, 512)
        key = jax.random.key(seed)
        k0, k1, k2, k3 = jax.random.split(key, 4)
        x = jax.random.normal(k0, (BATCH, SEQ, DMODEL), dtype=jnp.float32)
        Wr = jax.random.normal(k1, (DMODEL, N_EXPERTS), dtype=jnp.float32) * 0.02
        W1 = jax.random.normal(k2, (N_EXPERTS, DMODEL, DFF), dtype=jnp.float32) * 0.02
        W2 = jax.random.normal(k3, (N_EXPERTS, DFF, DMODEL), dtype=jnp.float32) * 0.02
        return {'x': x, 'Wr': Wr, 'W1': W1, 'W2': W2}
    _L0_ffn_all = _L0_ffn_setup()
    _L0_ffn_in = {k: v for k, v in _L0_ffn_all.items() if k in ('Wr', 'W1', 'W2')}
    del _L0_ffn_all

    def _L1_attn_setup():
        import math
        import jax, jax.numpy as jnp
        import numpy as np
        N_HEADS = 16
        D_EMBED = 128
        key = jax.random.key(seed)
        ks = jax.random.split(key, 5)
        b, l, d = (2, 256, D_EMBED)
        return {'x': jax.random.normal(ks[0], (b, l, d), dtype=jnp.float32), 'w_in': jax.random.normal(ks[1], (3 * d, d), dtype=jnp.float32) * 0.02, 'b_in': jax.random.normal(ks[2], (3 * d,), dtype=jnp.float32) * 0.02, 'w_out': jax.random.normal(ks[3], (d, d), dtype=jnp.float32) * 0.02, 'b_out': jax.random.normal(ks[4], (d,), dtype=jnp.float32) * 0.02}
    _L1_attn_all = _L1_attn_setup()
    _L1_attn_in = {k: v for k, v in _L1_attn_all.items() if k in ('w_in', 'b_in', 'w_out', 'b_out')}
    del _L1_attn_all

    def _L1_xattn_setup():
        import jax, jax.numpy as jnp
        import numpy as np
        DIM = 128
        HEADS = 16
        DIM_HEAD = 64
        SCALE = DIM_HEAD ** (-0.5)
        EPS = 1e-05

        def stable_layernorm(x, g):
            x = x / jax.lax.stop_gradient(jnp.max(x, axis=-1, keepdims=True))
            mean = jnp.mean(x, axis=-1, keepdims=True)
            var = jnp.mean(jnp.square(x - mean), axis=-1, keepdims=True)
            return (x - mean) * jax.lax.rsqrt(var + EPS) * g
        key = jax.random.key(seed)
        ks = jax.random.split(key, 6)
        b, n, m = (4, 256, 256)
        inner = HEADS * DIM_HEAD
        return {'x': jax.random.normal(ks[0], (b, n, DIM), jnp.float32), 'context': jax.random.normal(ks[1], (b, m, DIM), jnp.float32), 'Wq': jax.random.normal(ks[2], (DIM, inner), jnp.float32) * 0.02, 'Wkv': jax.random.normal(ks[3], (DIM, 2 * inner), jnp.float32) * 0.02, 'Wo': jax.random.normal(ks[4], (inner, DIM), jnp.float32) * 0.02, 'g_in': jnp.ones((DIM,), jnp.float32), 'g_out': jnp.ones((DIM,), jnp.float32), 'null_kv': jax.random.normal(ks[5], (2, DIM_HEAD), jnp.float32)}
    _L1_xattn_all = _L1_xattn_setup()
    _L1_xattn_in = {k: v for k, v in _L1_xattn_all.items() if k in ('Wq', 'Wkv', 'Wo', 'g_in', 'g_out', 'null_kv')}
    del _L1_xattn_all

    def _L1_ffn_setup():
        import jax, jax.numpy as jnp
        import numpy as np
        H = 128
        M = 64
        E = 16
        TOP_K = 2
        SCALE = 2.5
        NORM_TOPK = True
        B, S = (1, 128)

        def _moe(x, gate_w, w_gate, w_up, w_down, ws_gate, ws_up, ws_down):
            T = x.shape[0]
            shared = jax.nn.silu(x @ ws_gate) * (x @ ws_up) @ ws_down
            scores = jax.nn.sigmoid(x.astype(jnp.float32) @ gate_w.T.astype(jnp.float32))
            topk_w, topk_idx = jax.lax.top_k(scores, TOP_K)
            if NORM_TOPK and TOP_K > 1:
                topk_w = topk_w / (topk_w.sum(-1, keepdims=True) + 1e-20)
            topk_w = topk_w * SCALE
            route = jnp.zeros((T, E), topk_w.dtype).at[jnp.arange(T)[:, None], topk_idx].set(topk_w)
            g = jnp.einsum('th,ehm->etm', x, w_gate)
            u = jnp.einsum('th,ehm->etm', x, w_up)
            eo = jnp.einsum('etm,emh->eth', jax.nn.silu(g) * u, w_down)
            routed = jnp.einsum('te,eth->th', route.astype(x.dtype), eo)
            return routed + shared
        key = jax.random.key(seed)
        ks = jax.random.split(key, 8)
        std = 0.02
        return {'hidden_states': jax.random.normal(ks[0], (B, S, H), jnp.float32), 'gate_w': jax.random.normal(ks[1], (E, H), jnp.float32) * std, 'w_gate': jax.random.normal(ks[2], (E, H, M), jnp.float32) * std, 'w_up': jax.random.normal(ks[3], (E, H, M), jnp.float32) * std, 'w_down': jax.random.normal(ks[4], (E, M, H), jnp.float32) * std, 'ws_gate': jax.random.normal(ks[5], (H, M), jnp.float32) * std, 'ws_up': jax.random.normal(ks[6], (H, M), jnp.float32) * std, 'ws_down': jax.random.normal(ks[7], (M, H), jnp.float32) * std}
    _L1_ffn_all = _L1_ffn_setup()
    _L1_ffn_in = {k: v for k, v in _L1_ffn_all.items() if k in ('gate_w', 'w_gate', 'w_up', 'w_down', 'ws_gate', 'ws_up', 'ws_down')}
    del _L1_ffn_all
    return {'x': x, 'ctx_1024': ctx_1024, 'L0_attn_Wq': _L0_attn_in['Wq'], 'L0_attn_bq': _L0_attn_in['bq'], 'L0_attn_Wk': _L0_attn_in['Wk'], 'L0_attn_bk': _L0_attn_in['bk'], 'L0_attn_Wv': _L0_attn_in['Wv'], 'L0_attn_bv': _L0_attn_in['bv'], 'L0_attn_Wr': _L0_attn_in['Wr'], 'L0_attn_br': _L0_attn_in['br'], 'L0_attn_Wo': _L0_attn_in['Wo'], 'L0_attn_bo': _L0_attn_in['bo'], 'L0_xattn_Wq': _L0_xattn_in['Wq'], 'L0_xattn_Wk': _L0_xattn_in['Wk'], 'L0_xattn_Wv': _L0_xattn_in['Wv'], 'L0_xattn_Wk_ip': _L0_xattn_in['Wk_ip'], 'L0_xattn_Wv_ip': _L0_xattn_in['Wv_ip'], 'L0_xattn_Wo': _L0_xattn_in['Wo'], 'L0_xattn_bo': _L0_xattn_in['bo'], 'L0_ffn_Wr': _L0_ffn_in['Wr'], 'L0_ffn_W1': _L0_ffn_in['W1'], 'L0_ffn_W2': _L0_ffn_in['W2'], 'L1_attn_w_in': _L1_attn_in['w_in'], 'L1_attn_b_in': _L1_attn_in['b_in'], 'L1_attn_w_out': _L1_attn_in['w_out'], 'L1_attn_b_out': _L1_attn_in['b_out'], 'L1_xattn_Wq': _L1_xattn_in['Wq'], 'L1_xattn_Wkv': _L1_xattn_in['Wkv'], 'L1_xattn_Wo': _L1_xattn_in['Wo'], 'L1_xattn_g_in': _L1_xattn_in['g_in'], 'L1_xattn_g_out': _L1_xattn_in['g_out'], 'L1_xattn_null_kv': _L1_xattn_in['null_kv'], 'L1_ffn_gate_w': _L1_ffn_in['gate_w'], 'L1_ffn_w_gate': _L1_ffn_in['w_gate'], 'L1_ffn_w_up': _L1_ffn_in['w_up'], 'L1_ffn_w_down': _L1_ffn_in['w_down'], 'L1_ffn_ws_gate': _L1_ffn_in['ws_gate'], 'L1_ffn_ws_up': _L1_ffn_in['ws_up'], 'L1_ffn_ws_down': _L1_ffn_in['ws_down']}

def reference(x, ctx_1024, L0_attn_Wq, L0_attn_bq, L0_attn_Wk, L0_attn_bk, L0_attn_Wv, L0_attn_bv, L0_attn_Wr, L0_attn_br, L0_attn_Wo, L0_attn_bo, L0_xattn_Wq, L0_xattn_Wk, L0_xattn_Wv, L0_xattn_Wk_ip, L0_xattn_Wv_ip, L0_xattn_Wo, L0_xattn_bo, L0_ffn_Wr, L0_ffn_W1, L0_ffn_W2, L1_attn_w_in, L1_attn_b_in, L1_attn_w_out, L1_attn_b_out, L1_xattn_Wq, L1_xattn_Wkv, L1_xattn_Wo, L1_xattn_g_in, L1_xattn_g_out, L1_xattn_null_kv, L1_ffn_gate_w, L1_ffn_w_gate, L1_ffn_w_up, L1_ffn_w_down, L1_ffn_ws_gate, L1_ffn_ws_up, L1_ffn_ws_down):
    import jax
    import jax.numpy as jnp

    def _L0_attn_ref(x, Wq, bq, Wk, bk, Wv, bv, Wr, br, Wo, bo):
        import jax, jax.numpy as jnp
        import numpy as np
        import math
        D_MODEL = 128
        N_HEADS = 16
        HEAD_DIM = D_MODEL // N_HEADS
        ROT_DIM = min(32, D_MODEL // 4)

        def _xavier(key, fan_in, fan_out):
            lim = math.sqrt(6.0 / (fan_in + fan_out))
            return jax.random.uniform(key, (fan_in, fan_out), jnp.float32, -lim, lim)
        B, S, _ = x.shape
        H, Dh, Dr = (N_HEADS, HEAD_DIM, ROT_DIM)
        q = (x @ Wq + bq).reshape(B, S, H, Dh)
        k = (x @ Wk + bk).reshape(B, S, H, Dh)
        v = (x @ Wv + bv).reshape(B, S, H, Dh)
        r = (x @ Wr + br).reshape(B, S, H, Dr)
        q = jnp.concatenate([q, r], axis=-1)
        k = jnp.concatenate([k, r], axis=-1)
        scale = 1.0 / math.sqrt(Dh + Dr)
        scores = jnp.einsum('bqhd,bkhd->bhqk', q * scale, k)
        attn = jax.nn.softmax(scores, axis=-1)
        out = jnp.einsum('bhqk,bkhd->bqhd', attn, v).reshape(B, S, H * Dh)
        return out @ Wo + bo

    def _L0_xattn_ref(x, context, Wq, Wk, Wv, Wk_ip, Wv_ip, Wo, bo):
        import jax, jax.numpy as jnp
        import numpy as np
        HEADS = 16
        DIM_HEAD = 64
        INNER = HEADS * DIM_HEAD
        QUERY_DIM = 128
        CONTEXT_DIM = 128
        TEXT_LEN = 77
        IMG_SCALE = 1.0
        SCALE = DIM_HEAD ** (-0.5)

        def _attend(q, k, v):
            sim = jnp.einsum('bihd,bjhd->bhij', q, k) * SCALE
            attn = jax.nn.softmax(sim, axis=-1)
            out = jnp.einsum('bhij,bjhd->bihd', attn, v)
            B, N, H, D = out.shape
            return out.reshape(B, N, H * D)
        B, N, _ = x.shape
        ctx_txt = context[:, :TEXT_LEN, :]
        ctx_img = context[:, TEXT_LEN:, :]
        q = (x @ Wq).reshape(B, N, HEADS, DIM_HEAD)
        k = (ctx_txt @ Wk).reshape(B, TEXT_LEN, HEADS, DIM_HEAD)
        v = (ctx_txt @ Wv).reshape(B, TEXT_LEN, HEADS, DIM_HEAD)
        out = _attend(q, k, v)
        Li = ctx_img.shape[1]
        k_ip = (ctx_img @ Wk_ip).reshape(B, Li, HEADS, DIM_HEAD)
        v_ip = (ctx_img @ Wv_ip).reshape(B, Li, HEADS, DIM_HEAD)
        out_ip = _attend(q, k_ip, v_ip)
        out = out + IMG_SCALE * out_ip
        return out @ Wo + bo

    def _L0_ffn_ref(x, Wr, W1, W2):
        import jax, jax.numpy as jnp
        import numpy as np
        N_EXPERTS = 8
        CAP_FACTOR = 1.25
        BATCH, SEQ, DMODEL, DFF = (4, 256, 128, 512)
        B, S, D = x.shape
        E = W1.shape[0]
        cap = int(CAP_FACTOR * B * S / E)
        t = x.reshape(-1, D)
        probs = jax.nn.softmax(t @ Wr, axis=-1)
        idx = jnp.argmax(probs, axis=-1)
        pmax = jnp.max(probs, axis=-1)
        onehot = jax.nn.one_hot(idx, E, dtype=jnp.int32)
        pos = jnp.sum(jnp.cumsum(onehot, axis=0) * onehot, axis=-1) - 1
        kept = pos < cap
        flat = idx * cap + jnp.minimum(pos, cap - 1)
        disp = jnp.zeros((E * cap, D), t.dtype).at[flat].add(t * kept[:, None].astype(t.dtype))
        ein = disp.reshape(E, cap, D)
        h = jax.nn.relu(jnp.einsum('ecd,edf->ecf', ein, W1))
        eout = jnp.einsum('ecf,efd->ecd', h, W2).reshape(E * cap, D)
        comb = jnp.where(kept[:, None], eout[flat], t)
        factor = jnp.where(kept, pmax, jnp.ones_like(pmax))
        out = (comb * factor[:, None]).reshape(B, S, D)
        return out

    def _L1_attn_ref(x, w_in, b_in, w_out, b_out):
        import math
        import jax, jax.numpy as jnp
        import numpy as np
        N_HEADS = 16
        D_EMBED = 128
        b, l, d = x.shape
        h = N_HEADS
        scale = 1.0 / math.sqrt(d // h)
        x_proj = (x @ w_in.T + b_in).reshape(b, l, h, -1)
        q, k, v = jnp.split(x_proj, 3, axis=-1)
        att = jnp.einsum('blhd,bmhd->blmh', q, k) * scale
        att = jax.nn.softmax(att, axis=2)
        opt = jnp.einsum('blmh,blhd->blhd', att, v).reshape(b, l, d)
        return opt @ w_out.T + b_out

    def _L1_xattn_ref(x, context, Wq, Wkv, Wo, g_in, g_out, null_kv):
        import jax, jax.numpy as jnp
        import numpy as np
        DIM = 128
        HEADS = 16
        DIM_HEAD = 64
        SCALE = DIM_HEAD ** (-0.5)
        EPS = 1e-05

        def stable_layernorm(x, g):
            x = x / jax.lax.stop_gradient(jnp.max(x, axis=-1, keepdims=True))
            mean = jnp.mean(x, axis=-1, keepdims=True)
            var = jnp.mean(jnp.square(x - mean), axis=-1, keepdims=True)
            return (x - mean) * jax.lax.rsqrt(var + EPS) * g
        b, n, _ = x.shape
        x = stable_layernorm(x, g_in)
        q = x @ Wq
        kv = context @ Wkv
        k, v = jnp.split(kv, 2, axis=-1)

        def to_heads(t):
            return t.reshape(b, t.shape[1], HEADS, DIM_HEAD).transpose(0, 2, 1, 3)
        q, k, v = (to_heads(q), to_heads(k), to_heads(v))
        nk = jnp.broadcast_to(null_kv[0], (b, HEADS, 1, DIM_HEAD))
        nv = jnp.broadcast_to(null_kv[1], (b, HEADS, 1, DIM_HEAD))
        k = jnp.concatenate([nk, k], axis=2)
        v = jnp.concatenate([nv, v], axis=2)
        q = q * SCALE
        sim = jnp.einsum('bhid,bhjd->bhij', q, k)
        attn = jax.nn.softmax(sim.astype(jnp.float32), axis=-1).astype(sim.dtype)
        out = jnp.einsum('bhij,bhjd->bhid', attn, v)
        out = out.transpose(0, 2, 1, 3).reshape(b, n, HEADS * DIM_HEAD)
        out = out @ Wo
        return stable_layernorm(out, g_out)

    def _L1_ffn_ref(hidden_states, gate_w, w_gate, w_up, w_down, ws_gate, ws_up, ws_down):
        import jax, jax.numpy as jnp
        import numpy as np
        H = 128
        M = 64
        E = 16
        TOP_K = 2
        SCALE = 2.5
        NORM_TOPK = True
        B, S = (1, 128)

        def _moe(x, gate_w, w_gate, w_up, w_down, ws_gate, ws_up, ws_down):
            T = x.shape[0]
            shared = jax.nn.silu(x @ ws_gate) * (x @ ws_up) @ ws_down
            scores = jax.nn.sigmoid(x.astype(jnp.float32) @ gate_w.T.astype(jnp.float32))
            topk_w, topk_idx = jax.lax.top_k(scores, TOP_K)
            if NORM_TOPK and TOP_K > 1:
                topk_w = topk_w / (topk_w.sum(-1, keepdims=True) + 1e-20)
            topk_w = topk_w * SCALE
            route = jnp.zeros((T, E), topk_w.dtype).at[jnp.arange(T)[:, None], topk_idx].set(topk_w)
            g = jnp.einsum('th,ehm->etm', x, w_gate)
            u = jnp.einsum('th,ehm->etm', x, w_up)
            eo = jnp.einsum('etm,emh->eth', jax.nn.silu(g) * u, w_down)
            routed = jnp.einsum('te,eth->th', route.astype(x.dtype), eo)
            return routed + shared
        b, s, h = hidden_states.shape
        x = hidden_states.reshape(-1, h)
        out = _moe(x, gate_w, w_gate, w_up, w_down, ws_gate, ws_up, ws_down)
        return out.reshape(b, s, h)
    x = _layernorm(x + _L0_attn_ref(x, L0_attn_Wq, L0_attn_bq, L0_attn_Wk, L0_attn_bk, L0_attn_Wv, L0_attn_bv, L0_attn_Wr, L0_attn_br, L0_attn_Wo, L0_attn_bo), axis=-1)
    x = _layernorm(x + _L0_xattn_ref(x, ctx_1024, L0_xattn_Wq, L0_xattn_Wk, L0_xattn_Wv, L0_xattn_Wk_ip, L0_xattn_Wv_ip, L0_xattn_Wo, L0_xattn_bo), axis=-1)
    x = _layernorm(x + _L0_ffn_ref(x, L0_ffn_Wr, L0_ffn_W1, L0_ffn_W2), axis=-1)
    x = _layernorm(x + _L1_attn_ref(x, L1_attn_w_in, L1_attn_b_in, L1_attn_w_out, L1_attn_b_out), axis=-1)
    x = _layernorm(x + _L1_xattn_ref(x, ctx_1024, L1_xattn_Wq, L1_xattn_Wkv, L1_xattn_Wo, L1_xattn_g_in, L1_xattn_g_out, L1_xattn_null_kv), axis=-1)
    x = _layernorm(x + _L1_ffn_ref(x, L1_ffn_gate_w, L1_ffn_w_gate, L1_ffn_w_up, L1_ffn_w_down, L1_ffn_ws_gate, L1_ffn_ws_up, L1_ffn_ws_down), axis=-1)
    return x

_drawn_inputs = setup_inputs


def setup_inputs(seed=0):
    import zlib

    import numpy as np

    out = dict(_drawn_inputs(seed))
    spreads = {'L0_attn_bq': (0.0, 0.8),
     'L0_attn_bk': (0.0, 0.8),
     'L0_attn_bv': (0.0, 0.1),
     'L0_attn_br': (0.0, 0.8),
     'L0_attn_bo': (0.0, 0.1),
     'L0_xattn_bo': (0.0, 0.1),
     'L1_xattn_g_in': (1.0, 0.6),
     'L1_xattn_g_out': (1.0, 0.2)}
    factors = {'L0_ffn_Wr': 7.155,
     'L0_ffn_W1': 8.0,
     'L0_ffn_W2': 6.936,
     'L1_attn_b_in': 8.0,
     'L1_attn_b_out': 3.993,
     'L1_ffn_gate_w': 7.66,
     'L1_ffn_w_gate': 7.697,
     'L1_ffn_w_up': 7.433,
     'L1_ffn_w_down': 7.433,
     'L1_ffn_ws_gate': 8.0,
     'L1_ffn_ws_up': 8.0,
     'L1_ffn_ws_down': 8.0}
    for name, (base, spread) in spreads.items():
        noise = np.random.default_rng([zlib.crc32(name.encode()), seed]).standard_normal(out[name].shape)
        drawn = base * np.exp(spread * noise) if base else spread * noise
        out[name] = jnp.asarray(drawn.astype(out[name].dtype))
    for name, factor in factors.items():
        out[name] = (out[name] * factor).astype(out[name].dtype)
    return out
```

```python
from contextlib import ExitStack

import numpy as np

import concourse.bass as bass
from concourse import mybir

F32 = mybir.dt.float32
BF16 = mybir.dt.bfloat16
U32 = mybir.dt.uint32
ALU = mybir.AluOpType
ACT = mybir.ActivationFunctionType
AX_X = mybir.AxisListType.X

P = 128
BATCHES = 8
TOKENS = 128
D = 128
HEADS = 16
GROUP = 4
GROUPS = HEADS // GROUP
CTX = 77
XD = 64
VD = 8
LN_EPS = 1e-5
BANK = 512

EXPERTS = 8
CAP = int(1.25 * BATCHES * TOKENS / EXPERTS)
SLOTS = EXPERTS * CAP
HALF = CAP // 2
FB = 4

E2 = 16
M2 = 64
ROUTE_SCALE = 2.5

LAYERS = (
    dict(blocks=8, rows=40, step=64, scale=1.0 / (8 + 32) ** 0.5, keys=CTX, stable=False, own_values=False),
    dict(blocks=4, rows=8, step=32, scale=1.0 / 8 ** 0.5, keys=CTX + 1, stable=True, own_values=True),
)
X_SCALE = XD ** -0.5


def columns(*parts):
    at, out = 0, {}
    for name, width in parts:
        out[name] = (at, at + width)
        at += width
    return out, at


def attn_columns(layer):
    n = LAYERS[layer]["blocks"]
    return columns(("wq", n * P), ("wk", n * P), ("wv", D), ("wo", D), ("bv", D), ("bo", D), ("bq", n), ("bk", n))


X_COLS = columns(("wq", 1024), ("wk", 1024), ("wv", 1024), ("wo", 1024), ("row", D), ("col", 1), ("null", 1))
GU = E2 * M2 + M2
F_COLS = columns(("wg", E2 * M2), ("wu", E2 * M2), ("ws", 2 * M2), ("wd", 9 * D), ("gate", E2))
C_COLS = columns(("ident", P), ("rev8", BATCHES * EXPERTS), ("rev16", E2), ("token", BATCHES), ("wr", EXPERTS),
                 ("tri", P))


class Unit:

    def __init__(self, kind, batch, group, b, c):
        self.kind, self.batch, self.group, self.b, self.c = kind, batch, group, b, c
        self.par = c % 2

    def count(self, back=0):
        return self.b * 8 + (self.c + 1 - back)

    def half(self):
        return self.b * 4 + (self.c // 2 + 1)


CREDIT = 2


def turns(layer, u, back=0):
    if not LAYERS[layer]["own_values"]:
        return u.count(back)
    return u.batch * GROUPS + (u.group + 1 + CREDIT - back)


def half_turns(layer, u):
    if not LAYERS[layer]["own_values"]:
        return u.half()
    return u.batch * (GROUPS // 2) + (u.group // 2 + 1 + CREDIT // 2)


def has_turned(layer, u):
    return LAYERS[layer]["own_values"] or not isinstance(u.b, int) or u.c >= 2


def heads_of(layer, u):
    per = P // LAYERS[layer]["step"] if u.kind == "a" else P // XD
    first = u.group % per + per * GROUP * (u.group // per)
    return range(first, first + per * GROUP, per)


class Job:

    def __init__(self, name, batch, b=0, c=0, per=0, before=None):
        self.name, self.batch, self.b, self.c, self.per, self.before = name, batch, b, c, per, before
        self.par = c % 2

    def count(self):
        return self.b * self.per + (self.c + 1)


def job_names(layer):
    n = LAYERS[layer]["blocks"] // 4
    qa = [f"qa{i}" for i in range(n)]
    ka = [f"ka{i}" for i in range(n)]
    return qa, ka, ["qx0", "qx1"], ["kx0", "kx1"], ["vx0", "vx1"], ["tx0", "tx1"]


def before_loop(layer):
    qa, ka, qx, kx, vx, tx = job_names(layer)
    return [[("xa", 0)] + [(n, 0) for n in qa + ka] + [("va", 0)],
            [], [(n, 0) for n in kx], [("xa", 1)], [(n, 1) for n in qa + ka],
            [], [], [("va", 1)], [("ta", 0), ("ya", 0), ("xx", 0)] + [(n, 0) for n in qx]]


def in_loop(layer):
    qa, ka, qx, kx, vx, tx = job_names(layer)
    return [[(n, 0) for n in vx], [("xa", 2)], [(n, 2) for n in qa + ka], [("va", 2), ("ta", 1)],
            [("ya", 1)], [(n, 1) for n in kx], [("xx", 1)], [(n, 0) for n in tx] + [("yx", 0)] + [(n, 1) for n in qx]]


def after_loop(layer):
    qa, ka, qx, kx, vx, tx = job_names(layer)
    return [[(n, 6) for n in vx], [], [], [("ta", 7), ("ya", 7)] + [(n, 7) for n in kx] + [("xx", 7)] + [(n, 7) for n in qx],
            [], [], [(n, 7) for n in vx] + [(n, 6) for n in tx], [("yx", 6)],
            [], [], [(n, 7) for n in tx] + [("yx", 7)]]


PER_LOOP = [sum(map(len, in_loop(layer))) for layer in range(2)]
LOOPS = BATCHES - 2


def numbered(layer, slots, first, b, before):
    out, made = [], list(before)
    for slot in slots:
        out.append([])
        for name, k in slot:
            made.append(Job(name, b + k, b, first + len(made) - 2, PER_LOOP[layer], made[-2]))
            out[-1].append(made[-1])
    return out


def slots_before(layer):
    units = [Unit("a", k, g, 0, 4 * k + g) for k in range(2) for g in range(GROUPS)]
    jobs = numbered(layer, before_loop(layer), 0, 0, [None, None])
    return [(None, None, None, jobs[0])] + [
        (u, units[i - 2] if i >= 2 else None, units[i - 3] if i >= 3 else None, jobs[i + 1])
        for i, u in enumerate(units)]


def slots_loop(layer, b):
    first = sum(map(len, before_loop(layer)))
    units = [Unit("a", b + 1, g, b, 4 + g) for g in range(1, GROUPS)]
    units += [Unit("x", b, g, b, 8 + g) for g in range(GROUPS)] + [Unit("a", b + 2, g, b, 12 + g) for g in range(GROUPS)]
    return [(units[i + 3], units[i + 1], units[i], jobs) for i, jobs in enumerate(numbered(layer, in_loop(layer), first, b, [Job("qx0", b), Job("qx1", b)]))]


def slots_after(layer):
    first = sum(map(len, before_loop(layer))) + LOOPS * PER_LOOP[layer]
    n = 8 * (BATCHES - 1)
    units = [Unit("a", 7, g, 0, n - 4 + g) for g in range(1, GROUPS)]
    units += [Unit("x", 6 + k, g, 0, n + 4 * k + g) for k in range(2) for g in range(GROUPS)] + [None] * 3
    return [(units[i + 3], units[i + 1], units[i], jobs) for i, jobs in enumerate(numbered(layer, after_loop(layer), first, 0, [Job("qx0", 6), Job("qx1", 6)]))]


def decoder(nc, x, ctx_t, consts, attn, cross, null_v, w1, w2, ffn, out):
    stack = ExitStack()
    with stack:
        def sb(name, shape, dt=F32):
            return stack.enter_context(nc.sbuf_tensor(name, shape, dt))

        def sem(name):
            return stack.enter_context(nc.semaphore(name))

        const_sb = sb("const_sb", [P, C_COLS[1]])
        attn_sb = [sb(f"attn_sb{n}", [P, attn_columns(n)[1]]) for n in range(2)]
        cross_sb = [sb(f"cross_sb{n}", [P, X_COLS[1]]) for n in range(2)]
        ffn_sb = sb("ffn_sb", [P, F_COLS[1]])

        def cut(tensor, table, name):
            a, b = table[0][name]
            return tensor[:, a:b]

        ident = cut(const_sb, C_COLS, "ident")

        def wa(layer, name):
            return cut(attn_sb[layer], attn_columns(layer), name)

        def wx(layer, name):
            return cut(cross_sb[layer], X_COLS, name)

        xres = sb("xres", [P, BATCHES, D])
        cur_a = sb("cur_a", [P, D])
        cur_x = sb("cur_x", [P, D])
        ctx_cur = sb("ctx_cur", [P, CTX])
        xt_a = sb("xt_a", [P, TOKENS])
        xt_x = sb("xt_x", [P, TOKENS])
        q_a = sb("q_a", [P, 8, TOKENS])
        k_a = sb("k_a", [P, 8, TOKENS])
        v_a = sb("v_a", [P, HEADS, VD + 1])
        q_x = sb("q_x", [P, 8, TOKENS])
        k_x = sb("k_x", [P, 8, CTX + 1])
        v_x = sb("v_x", [CTX + 1, HEADS, XD + 1])
        negmax = sb("negmax", [P, 2, GROUP])
        probs = sb("probs", [P, 2, GROUP, TOKENS])
        probs_t = sb("probs_t", [P, 2, GROUP, TOKENS])
        rsum = sb("rsum", [P, 2, GROUP])
        probs_a = sb("probs_a", [P, 2, GROUP, TOKENS])
        sums_a = sb("sums_a", [P, HEADS])
        inv_a = sb("inv_a", [P, HEADS])
        weight_a = sb("weight_a", [P, HEADS])
        mix_a = sb("mix_a", [P, HEADS, VD])
        mix_x = sb("mix_x", [P, HEADS, XD])
        mixt_a = sb("mixt_a", [P, TOKENS])
        mixt_x = sb("mixt_x", [P, 8, TOKENS])
        kb_scaled = sb("kb_scaled", [P, 8])
        y = {k: sb(f"y_{k}", [P, D]) for k in "ax"}
        bns = {k: sb(f"bns_{k}", [P, 6]) for k in "axsz"}
        mv = {k: sb(f"mv_{k}", [P, 2]) for k in "axsz"}
        rmax = {k: sb(f"rmax_{k}", [P, 1]) for k in "sz"}
        rinv = {k: sb(f"rinv_{k}", [P, 1]) for k in "sz"}
        ve = sb("ve", [P, 1])
        rstd = sb("rstd", [P, 1])
        r2 = sb("r2", [P, 1])
        rstd_r = sb("rstd_r", [P, 1])
        z = sb("z", [P, D])
        minus_half = sb("minus_half", [P, 1])
        normed = sb("normed", [P, D])

        x2t = sb("x2t", [P, BATCHES, TOKENS])
        lg = {n: sb(f"lg_{n}", [P, BATCHES, EXPERTS]) for n in ("centred", "exp", "pick", "onehot", "at")}
        onehot_b = sb("onehot_b", [P, BATCHES, EXPERTS], BF16)
        tri_b = sb("tri_b", [P, P], BF16)
        ones_b = sb("ones_b", [P, P], BF16)
        tok = {n: sb(f"tok_{n}", [P, BATCHES]) for n in ("max", "sum", "prob", "pick", "pos", "kept", "slot", "spare",
                                                           "apart", "put", "base", "lost", "own", "factor")}
        put_at = sb("put_at", [P, BATCHES], U32)
        get_at = sb("get_at", [P, BATCHES], U32)
        slot_in = sb("slot_in", [HALF, 2, 2, D])
        slot_t = sb("slot_t", [P, 2, CAP])
        w1_sb = sb("w1_sb", [P, 2, FB * P])
        w2_sb = sb("w2_sb", [P, 2, FB, D])
        hidden = sb("hidden", [P, FB, CAP])
        slot_out = sb("slot_out", [HALF, 2, 2, D])
        zeros = sb("zeros", [P, SLOTS])
        back = sb("back", [P, BATCHES, D])
        own = sb("own", [P, BATCHES, D])
        y8 = sb("y8", [P, BATCHES, D])
        bns8 = sb("bns8", [P, BATCHES, 6])
        mv8 = sb("mv8", [P, BATCHES, 2])
        ve8 = sb("ve8", [P, BATCHES])
        rstd8 = sb("rstd8", [P, BATCHES])
        half8 = sb("half8", [P, BATCHES])
        slots_dram = nc.dram_tensor("slots_dram", (SLOTS + BATCHES * TOKENS, D), F32).ap()
        outs_dram = nc.dram_tensor("outs_dram", (SLOTS, D), F32).ap()

        xt_f = sb("xt_f", [P, TOKENS])
        gate_sb = sb("gate_sb", [P, E2 + 2 * M2])
        tanh_g = sb("tanh_g", [P, 2, BANK])
        hid = sb("hid", [P, 2, BANK])
        hid_r = sb("hid_r", [P, 2, BANK])
        tanh_s = sb("tanh_s", [P, M2])
        hid_s = sb("hid_s", [P, M2])
        hid_s2 = sb("hid_s2", [P, M2])
        ht = sb("ht", [P, 8, TOKENS])
        ht_s = sb("ht_s", [M2, TOKENS])
        r16 = {n: sb(f"r16_{n}", [P, E2]) for n in ("exp", "score", "w1", "one1", "rest", "w2", "two", "sum", "route")}
        r1 = {n: sb(f"r1_{n}", [P, 1]) for n in ("m1", "x1", "m2", "x2", "sum", "inv")}
        y_f = sb("y_f", [P, D])
        out_sb = sb("out_sb", [P, D])

        bank = [stack.enter_context(nc.psum_tensor(f"bank{i}", [P, BANK], F32)) for i in range(8)]
        score_ps, flip_ps, value_ps, job_ps = bank[0:2], bank[2:4], bank[4:6], bank[6:8]
        up_ps = (score_ps, flip_ps)

        in_const, in_x = sem("in_const"), sem("in_x")
        in_attn = [sem(f"in_attn{n}") for n in range(2)]
        in_cross = [sem(f"in_cross{n}") for n in range(2)]
        in_null, in_ffn = sem("in_null"), sem("in_ffn")
        held = sem("held")
        ready_half, ready_ones, ready_kb = sem("ready_half"), sem("ready_ones"), sem("ready_kb")
        gp_chain = sem("gp_chain")
        out_done = sem("out_done")
        layer_done = [sem(f"layer_done{n}") for n in range(2)]

        def signals(prefix, names):
            return {name: sem(f"{prefix}_{name}") for name in names.split()}

        PER_LAYER = """scores maxed probs flipped flip_out_v flip_out_s values divided rsum job cur_a cur_x
            xt_a xt_x q_a k_a v_a q_x k_x v_x mixt_a mixt_x ctx biased y_a y_x st_a st_x mv_a mv_x normed_x gp_a gp_x"""
        OWN_VALUES = " st_s mv_s st_z mv_z ya2 gp_z summed weigh mixed"
        sig = [signals(f"layer{n}", PER_LAYER + OWN_VALUES * n) for n in range(2)]

        moe = signals("moe", """ready turned0 turned1 x2t logits centred exp onehot cum put cleared scattered
            w_in0 w_in1 slot_in0 slot_in1 flipped slot_t up relu_s relu_v down out_sb stored0 stored1 gathered own chain
            mv rstd gp done""")
        f = signals("ffn", """cur turned xt gate gate_sb up0 up1 tanh tanh_s exp hid hid_s route routed flip_s
            flip0 flip1 ht_s ht0 ht1 down y st mv normed chain w gp out""")

        def hold(eng, semaphore, value):
            eng.wait_ge(semaphore, value)
            eng.sem_inc(held, 1)

        def mm(out_ap, lhs, rhs, first=True, last=True):
            return nc.tensor.matmul(out_ap, lhs, rhs, start=first, stop=last)

        def static(v):
            return isinstance(v, int)

        def mixes(layer, u):
            return u.kind == "x" or not LAYERS[layer]["own_values"]

        def pe_unit_scores(pe, layer, s, u):
            cfg = LAYERS[layer]
            if u.group == 0:
                n = cfg["blocks"] // 4 if u.kind == "a" else 2
                pe.wait_ge(s["q_a"] if u.kind == "a" else s["q_x"], (u.batch + 1) * n)
                pe.wait_ge(s["k_a"] if u.kind == "a" else s["k_x"], (u.batch + 1) * n)
            if not static(u.b) or u.c >= 2:
                pe.wait_ge(s["probs"], u.count(2))
            for i, h in enumerate(heads_of(layer, u)):
                if u.kind == "a":
                    per = P // cfg["step"]
                    r, blk, n = cfg["step"] * (h % per), h // per, cfg["rows"]
                    q, k, keys = q_a[r:r + n, blk, :], k_a[r:r + n, blk, :], TOKENS
                else:
                    r, blk, keys = XD * (h % 2), h // 2, cfg["keys"]
                    q, k = q_x[r:r + XD, blk, :], k_x[r:r + XD, blk, 0:keys]
                last = mm(score_ps[u.par][:, i * P:i * P + keys], q, k)
            last.then_inc(s["scores"], 1)

        def pe_unit_flip(pe, layer, s, u):
            keys = TOKENS if u.kind == "a" else LAYERS[layer]["keys"]
            pe.wait_ge(s["probs"], u.count())
            if has_turned(layer, u):
                pe.wait_ge((s["flip_out_v"], s["flip_out_s"])[u.par], half_turns(layer, u) - 1)
            for i in range(GROUP):
                last = nc.tensor.transpose(flip_ps[u.par][0:keys, i * P:(i + 1) * P], probs[:, u.par, i, 0:keys], ident)
            last.then_inc(s["flipped"], 1)

        def pe_unit_values(pe, layer, s, u):
            keys, v, w = (TOKENS, v_a, VD + 1) if u.kind == "a" else (LAYERS[layer]["keys"], v_x, XD + 1)
            pe.wait_ge((s["flip_out_v"], s["flip_out_s"])[u.par], half_turns(layer, u))
            if u.group == 0:
                pe.wait_ge(s["v_a"] if u.kind == "a" else s["v_x"], (u.batch + 1) * (1 if u.kind == "a" else 2))
            if has_turned(layer, u):
                pe.wait_ge(s["divided"], turns(layer, u, 2))
            for i, h in enumerate(heads_of(layer, u)):
                last = mm(value_ps[u.par][:, i * w:(i + 1) * w], probs_t[0:keys, u.par, i, :], v[0:keys, h, :])
            last.then_inc(s["values"], 1)

        def read_out(layer, s, j):
            name, k = j.name, j.batch
            if name[0:2] in ("qa", "ka"):
                return (s["q_a"] if name[0] == "q" else s["k_a"]), k * (LAYERS[layer]["blocks"] // 4) + (int(name[2]) + 1)
            if name[0:2] in ("qx", "kx", "vx", "tx"):
                return {"q": s["q_x"], "k": s["k_x"], "v": s["v_x"], "t": s["mixt_x"]}[name[0]], k * 2 + (int(name[2]) + 1)
            if name == "yx" and LAYERS[layer]["stable"]:
                return s["y_x"], k * 2 + 1
            return {"xa": s["xt_a"], "xx": s["xt_x"], "va": s["v_a"], "ta": s["mixt_a"], "ya": s["y_a"], "yx": s["y_x"]}[name], k + 1

        def pe_job(pe, layer, s, j):
            cfg, ps, name, k = LAYERS[layer], job_ps[j.par], j.name, j.batch
            if j.before:
                pe.wait_ge(*read_out(layer, s, j.before))
            if name == "xa":
                pe.wait_ge(s["cur_a"], k + 1)
                last = nc.tensor.transpose(ps[:, 0:P], cur_a[:], ident)
            elif name == "xx":
                pe.wait_ge(s["cur_x"], k + 1)
                last = nc.tensor.transpose(ps[:, 0:P], cur_x[:], ident)
            elif name[0:2] in ("qa", "ka"):
                pe.wait_ge(s["xt_a"], k + 1)
                n = int(name[2])
                w = wa(layer, "w" + name[0])
                for i in range(4):
                    last = mm(ps[:, i * P:(i + 1) * P], w[:, (4 * n + i) * P:(4 * n + i + 1) * P], xt_a[:])
            elif name == "va":
                last = mm(ps[:, 0:D], xt_a[:], wa(layer, "wv"))
            elif name[0:2] == "qx":
                if static(k) and k == 0:
                    pe.wait_ge(in_cross[layer], 16)
                pe.wait_ge(s["xt_x"], k + 1)
                n = int(name[2])
                w = wx(layer, "wq")
                for i in range(4):
                    last = mm(ps[:, i * P:(i + 1) * P], w[:, (4 * n + i) * P:(4 * n + i + 1) * P], xt_x[:])
            elif name[0:2] == "kx":
                if static(k) and k == 0:
                    pe.wait_ge(in_cross[layer], 16)
                pe.wait_ge(s["ctx"], (k + 1) * 16)
                n = int(name[2])
                w = wx(layer, "wk")
                for i in range(4):
                    last = mm(ps[:, i * P:i * P + CTX], w[:, (4 * n + i) * P:(4 * n + i + 1) * P], ctx_cur[:])
            elif name[0:2] == "vx":
                n = int(name[2])
                last = mm(ps[0:CTX, :], ctx_cur[:], wx(layer, "wv")[:, n * BANK:(n + 1) * BANK])
            elif name == "ta":
                if cfg["own_values"]:
                    pe.wait_ge(s["mixed"], k + 1)
                else:
                    pe.wait_ge(s["divided"], 8 * k + 4 if static(k) and k == 0 else 8 * k)
                last = nc.tensor.transpose(ps[:, 0:P], mix_a[:, :, :].rearrange("p h d -> p (h d)"), ident)
            elif name[0:2] == "tx":
                if cfg["own_values"]:
                    pe.wait_ge(s["divided"], k * GROUPS + (GROUPS + CREDIT))
                else:
                    pe.wait_ge(s["divided"], 8 * k + 12 if not static(k) or k < 7 else 64)
                n = int(name[2])
                flat = mix_x[:, :, :].rearrange("p h d -> p (h d)")
                for i in range(4):
                    last = nc.tensor.transpose(ps[:, i * P:(i + 1) * P], flat[:, (4 * n + i) * P:(4 * n + i + 1) * P], ident)
            elif name == "ya":
                pe.wait_ge(s["mixt_a"], k + 1)
                last = mm(ps[:, 0:D], mixt_a[:], wa(layer, "wo"))
            elif name == "yx":
                pe.wait_ge(s["mixt_x"], (k + 1) * 2)
                w = wx(layer, "wo")
                for i in range(8):
                    last = mm(ps[:, 0:D], mixt_x[:, i, :], w[:, i * P:(i + 1) * P], i == 0, i == 7)
            last.then_inc(s["job"], 1)

        def pe_slot(pe, layer, s, scored, flipped, valued, jobs):
            if scored:
                pe_unit_scores(pe, layer, s, scored)
            if flipped and mixes(layer, flipped):
                pe_unit_flip(pe, layer, s, flipped)
            if valued and mixes(layer, valued):
                pe_unit_values(pe, layer, s, valued)
            for j in jobs:
                pe_job(pe, layer, s, j)

        def pe_layer(pe, layer):
            s = sig[layer]
            pe.wait_ge(in_const, 16)
            pe.wait_ge(in_attn[layer], 16)
            if LAYERS[layer]["own_values"]:
                for semaphore in (s["flipped"], s["values"]):
                    pe.sem_inc(semaphore, CREDIT)
            for slot in slots_before(layer):
                pe_slot(pe, layer, s, *slot)
            with pe.Fori(0, LOOPS) as b:
                for slot in slots_loop(layer, b):
                    pe_slot(pe, layer, s, *slot)
            for slot in slots_after(layer):
                pe_slot(pe, layer, s, *slot)

        def pe_experts(pe):
            pe.wait_ge(moe["ready"], 1)
            for i in range(BATCHES):
                last = nc.tensor.transpose(flip_ps[i // 4][:, (i % 4) * P:(i % 4 + 1) * P], xres[:, i, :], ident)
                if i % 4 == 3:
                    last.then_inc(moe["turned0"] if i == 3 else moe["turned1"], 1)
            pe.wait_ge(moe["x2t"], 2)
            for i in range(BATCHES):
                last = mm(value_ps[0][:, i * EXPERTS:(i + 1) * EXPERTS], x2t[:, i, :], cut(const_sb, C_COLS, "wr"))
            last.then_inc(moe["logits"], 1)
            pe.wait_ge(moe["onehot"], 1)
            cum = value_ps[1][:, 0:BATCHES * EXPERTS].rearrange("p (b e) -> p b e", b=BATCHES)
            mm(cum, tri_b[:], onehot_b[:, :, :], True, False)
            for i in range(BATCHES - 1):
                n = BATCHES - 1 - i
                last = mm(cum[:, i + 1:BATCHES, :], ones_b[:], onehot_b[:, i:i + 1, :].to_broadcast([P, n, EXPERTS]),
                          False, i == BATCHES - 2)
            last.then_inc(moe["cum"], 1)

            def turn(e, par):
                pe.wait_ge(moe["slot_in1"] if par else moe["slot_in0"], e * 8 + (2 - par) * 8)
                for t in range(2):
                    last = nc.tensor.transpose(job_ps[par][:, t * HALF:(t + 1) * HALF], slot_in[:, par, t, :],
                                               ident[0:HALF, 0:HALF])
                last.then_inc(moe["flipped"], 1)

            def up(e, par):
                pe.wait_ge(moe["slot_t"], e + 1)
                pe.wait_ge(moe["w_in1"] if par else moe["w_in0"], e * 16 + (2 - par) * 16)
                if not static(e) or e > 0:
                    pe.wait_ge(moe["relu_s"], e)
                    pe.wait_ge(moe["relu_v"], e)
                for fb in range(FB):
                    last = mm(score_ps[fb // 2][:, (fb % 2) * CAP:(fb % 2 + 1) * CAP], w1_sb[:, par, fb * P:(fb + 1) * P],
                              slot_t[:, par, :])
                    if fb % 2:
                        last.then_inc(moe["up"], 1)

            def down(e, par):
                pe.wait_ge(moe["relu_s"], e + 1)
                pe.wait_ge(moe["relu_v"], e + 1)
                if not static(e) or e > 1:
                    pe.wait_ge(moe["out_sb"], e - 1)
                for t in range(2):
                    for fb in range(FB):
                        last = mm(value_ps[par][0:HALF, t * D:(t + 1) * D], hidden[:, fb, t * HALF:(t + 1) * HALF],
                                  w2_sb[:, par, fb, :], fb == 0, fb == FB - 1)
                last.then_inc(moe["down"], 1)

            turn(0, 0)
            up(0, 0)
            turn(1, 1)
            down(0, 0)
            up(1, 1)
            turn(2, 0)
            down(1, 1)
            with pe.Fori(1, EXPERTS // 2 - 1) as i:
                up(i * 2, 0)
                turn(i * 2 + 1, 1)
                down(i * 2, 0)
                up(i * 2 + 1, 1)
                turn(i * 2 + 2, 0)
                down(i * 2 + 1, 1)
            up(EXPERTS - 2, 0)
            turn(EXPERTS - 1, 1)
            down(EXPERTS - 2, 0)
            up(EXPERTS - 1, 1)
            down(EXPERTS - 1, 1)

        def pe_ffn(pe):
            pe.wait_ge(in_ffn, 16)
            gate_w, ws = cut(ffn_sb, F_COLS, "gate"), cut(ffn_sb, F_COLS, "ws")
            wg, wu, wd = (cut(ffn_sb, F_COLS, n) for n in ("wg", "wu", "wd"))

            def turn(k):
                pe.wait_ge(f["cur"], k + 1)
                if not static(k) or k > 0:
                    pe.wait_ge(f["gate_sb"], k)
                nc.tensor.transpose(job_ps[0][:, 0:P], cur_a[:], ident).then_inc(f["turned"], 1)

            def up(k):
                pe.wait_ge(f["xt"], k + 1)
                mm(job_ps[0][:, 0:E2], xt_f[:], gate_w)
                mm(job_ps[0][:, E2:E2 + 2 * M2], xt_f[:], ws).then_inc(f["gate"], 1)
                for c in range(2):
                    if not static(k) or k > 0:
                        pe.wait_ge(f["hid"], k * 2 - 1 + c)
                    mm(up_ps[c][0][:, :], xt_f[:], wg[:, c * BANK:(c + 1) * BANK])
                    mm(up_ps[c][1][:, :], xt_f[:], wu[:, c * BANK:(c + 1) * BANK]).then_inc(f["up0"] if c == 0 else f["up1"], 1)

            def down(k):
                if not static(k) or k > 0:
                    pe.wait_ge(f["y"], k)
                hold(pe, f["hid_s"], k + 1)
                nc.tensor.transpose(job_ps[1][0:M2, D:D + P], hid_s2[:], ident).then_inc(f["flip_s"], 1)
                for c in range(2):
                    pe.wait_ge(f["routed"], k * 2 + (1 + c))
                    for i in range(4):
                        last = nc.tensor.transpose(value_ps[c][:, i * P:(i + 1) * P], hid_r[:, c, i * P:(i + 1) * P], ident)
                    last.then_inc(f["flip0"] if c == 0 else f["flip1"], 1)
                pe.wait_ge(f["ht_s"], k + 1)
                mm(job_ps[1][:, 0:D], ht_s[:], wd[0:M2, 8 * D:9 * D], True, False)
                for i in range(8):
                    if i % 4 == 0:
                        pe.wait_ge(f["ht1"] if i else f["ht0"], k + 1)
                    last = mm(job_ps[1][:, 0:D], ht[:, i, :], wd[:, i * D:(i + 1) * D], False, i == 7)
                last.then_inc(f["down"], 1)

            turn(0)
            up(0)
            turn(1)
            with pe.Fori(1, BATCHES - 1) as k:
                up(k)
                turn(k + 1)
                down(k - 1)
            up(BATCHES - 1)
            down(BATCHES - 2)
            down(BATCHES - 1)

        def act_unit_exp(act, layer, s, u):
            keys = TOKENS if u.kind == "a" else LAYERS[layer]["keys"]
            to = probs if mixes(layer, u) else probs_a
            act.wait_ge(s["maxed"], u.count())
            if not mixes(layer, u):
                act.wait_ge(s["summed"], turns(layer, u, 2))
            elif has_turned(layer, u):
                act.wait_ge(s["flipped"], turns(layer, u, 2))
            for i in range(GROUP):
                last = nc.scalar.activation(to[:, u.par, i, 0:keys], score_ps[u.par][:, i * P:i * P + keys], ACT.Exp,
                                            bias=negmax[:, u.par, i:i + 1])
            last.then_inc(s["probs"], 1)

        def act_unit_flip_out(act, layer, s, u):
            keys = TOKENS if u.kind == "a" else LAYERS[layer]["keys"]
            act.wait_ge(s["flipped"], turns(layer, u))
            if has_turned(layer, u):
                act.wait_ge(s["values"], turns(layer, u, 2))
            nc.scalar.copy(probs_t[0:keys, u.par, :, :],
                           flip_ps[u.par][0:keys, :].rearrange("p (h t) -> p h t", h=GROUP)).then_inc(s["flip_out_s"], 1)

        def act_job(act, layer, s, j):
            cfg, ps, name, k = LAYERS[layer], job_ps[j.par], j.name, j.batch
            if name not in ("xa", "xx", "ta", "tx0", "tx1", "ka0", "ka1", "kx0", "kx1"):
                return
            act.wait_ge(s["job"], j.count())
            blocks = ps[:, :].rearrange("p (n t) -> p n t", n=4)
            if name == "xa":
                done = nc.scalar.copy(xt_a[:], ps[:, 0:P]), s["xt_a"]
            elif name == "xx" and cfg["stable"]:
                done = nc.scalar.activation(xt_x[:], ps[:, 0:P], ACT.Copy, scale=wx(layer, "col")), s["xt_x"]
            elif name == "xx":
                done = nc.scalar.copy(xt_x[:], ps[:, 0:P]), s["xt_x"]
            elif name == "ta":
                done = nc.scalar.copy(mixt_a[:], ps[:, 0:P]), s["mixt_a"]
            elif name[0:2] == "tx":
                n = int(name[2])
                done = nc.scalar.copy(mixt_x[:, 4 * n:4 * n + 4, :], blocks), s["mixt_x"]
            elif name[0:2] == "ka":
                n = int(name[2])
                for i in range(4):
                    last = nc.scalar.activation(k_a[:, 4 * n + i, :], blocks[:, i, :], ACT.Identity, scale=cfg["scale"],
                                                bias=kb_scaled[:, 4 * n + i:4 * n + i + 1])
                done = last, s["k_a"]
            else:
                n = int(name[2])
                done = nc.scalar.mul(k_x[:, 4 * n:4 * n + 4, 0:CTX], blocks[:, :, 0:CTX], X_SCALE), s["k_x"]
            done[0].then_inc(done[1], 1)

        def act_slot(act, layer, s, scored, flipped, valued, jobs):
            if scored:
                act_unit_exp(act, layer, s, scored)
            if flipped and flipped.par == 1 and mixes(layer, flipped):
                act_unit_flip_out(act, layer, s, flipped)
            for j in jobs:
                act_job(act, layer, s, j)

        def act_layer(act, layer):
            s = sig[layer]
            act.wait_ge(ready_kb, layer + 1)
            if LAYERS[layer]["own_values"]:
                act.sem_inc(s["flip_out_s"], CREDIT // 2)
            for slot in slots_before(layer):
                act_slot(act, layer, s, *slot)
            with act.Fori(0, LOOPS) as b:
                for slot in slots_loop(layer, b):
                    act_slot(act, layer, s, *slot)
            for slot in slots_after(layer):
                act_slot(act, layer, s, *slot)

        def act_experts(act):
            for i in range(2):
                act.wait_ge(moe["turned1"] if i else moe["turned0"], 1)
                nc.scalar.copy(x2t[:, 4 * i:4 * i + 4, :], flip_ps[i][:, :].rearrange("p (b t) -> p b t", b=4)).then_inc(moe["x2t"], 1)
            act.wait_ge(moe["centred"], 1)
            nc.scalar.activation(lg["exp"][:], lg["centred"][:], ACT.Exp).then_inc(moe["exp"], 1)

            def one(e, par):
                act.wait_ge(moe["flipped"], e + 1)
                nc.scalar.copy(slot_t[:, par, :], job_ps[par][:, 0:CAP]).then_inc(moe["slot_t"], 1)

            def relu(e):
                act.wait_ge(moe["up"], e * 2 + 1)
                if not static(e) or e > 0:
                    act.wait_ge(moe["down"], e)
                nc.scalar.activation(hidden[:, 0:2, :], score_ps[0][:, 0:2 * CAP].rearrange("p (n t) -> p n t", n=2), ACT.Relu)\
                    .then_inc(moe["relu_s"], 1)

            one(0, 0)
            relu(0)
            one(1, 1)
            with act.Fori(0, EXPERTS // 2 - 1) as i:
                relu(i * 2 + 1)
                one(i * 2 + 2, 0)
                relu(i * 2 + 2)
                one(i * 2 + 3, 1)
            relu(EXPERTS - 1)

        def act_ffn(act):
            def turn(k):
                act.wait_ge(f["turned"], k + 1)
                nc.scalar.copy(xt_f[:], job_ps[0][:, 0:P]).then_inc(f["xt"], 1)

            def squash(k):
                act.wait_ge(f["gate_sb"], k + 1)
                nc.scalar.activation(r16["exp"][:], gate_sb[:, 0:E2], ACT.Exp, scale=-1.0).then_inc(f["exp"], 1)
                nc.scalar.activation(tanh_s[:], gate_sb[:, E2:E2 + M2], ACT.Tanh, scale=0.5).then_inc(f["tanh_s"], 1)
                for c in range(2):
                    act.wait_ge(f["up1"] if c else f["up0"], k + 1)
                    nc.scalar.activation(tanh_g[:, c, :], up_ps[c][0][:, :], ACT.Tanh, scale=0.5).then_inc(f["tanh"], 1)

            def flip(k):
                act.wait_ge(f["flip_s"], k + 1)
                nc.scalar.copy(ht_s[:], job_ps[1][0:M2, D:D + P]).then_inc(f["ht_s"], 1)
                for c in range(2):
                    act.wait_ge(f["flip1"] if c else f["flip0"], k + 1)
                    nc.scalar.copy(ht[:, 4 * c:4 * c + 4, :], value_ps[c][:, :].rearrange("p (n t) -> p n t", n=4))\
                        .then_inc(f["ht1"] if c else f["ht0"], 1)

            turn(0)
            squash(0)
            turn(1)
            with act.Fori(1, BATCHES - 1) as k:
                squash(k)
                turn(k + 1)
                flip(k - 1)
            squash(BATCHES - 1)
            flip(BATCHES - 2)
            flip(BATCHES - 1)

        def dve_unit_max(dve, layer, s, u):
            keys = TOKENS if u.kind == "a" else LAYERS[layer]["keys"]
            dve.wait_ge(s["scores"], u.count())
            nc.vector.tensor_reduce(negmax[:, u.par, :],
                                    score_ps[u.par][:, :].rearrange("p (h k) -> p h k", h=GROUP)[:, :, 0:keys],
                                    axis=AX_X, op=ALU.max, negate=True).then_inc(s["maxed"], 1)

        def dve_unit_flip_out(dve, layer, s, u):
            keys = TOKENS if u.kind == "a" else LAYERS[layer]["keys"]
            dve.wait_ge(s["flipped"], turns(layer, u))
            if has_turned(layer, u):
                dve.wait_ge(s["values"], turns(layer, u, 2))
            nc.vector.tensor_copy(probs_t[0:keys, u.par, :, :],
                                  flip_ps[u.par][0:keys, :].rearrange("p (h t) -> p h t", h=GROUP)).then_inc(s["flip_out_v"], 1)

        def dve_unit_sum(dve, layer, s, u):
            hs = heads_of(layer, u)
            dve.wait_ge(s["probs"], u.count())
            nc.vector.tensor_reduce(sums_a[:, hs.start:hs[-1] + 1:hs.step], probs_a[:, u.par, :, :], axis=AX_X, op=ALU.add)\
                .then_inc(s["summed"], 1)

        def dve_own_values(dve, s, u):
            k = u.batch
            dve.wait_ge(s["summed"], k * GROUPS + (GROUPS + CREDIT))
            nc.vector.reciprocal(inv_a[:], sums_a[:]).then_inc(s["weigh"], 1)
            dve.wait_ge(s["weigh"], k * 2 + 1)
            nc.vector.tensor_tensor(weight_a[:], sums_a[:], inv_a[:], ALU.mult).then_inc(s["weigh"], 1)
            if not static(k) or k > 0:
                dve.wait_ge(s["mixt_a"], k)
            dve.wait_ge(s["v_a"], k + 1)
            dve.wait_ge(s["weigh"], k * 2 + 2)
            nc.vector.tensor_tensor(mix_a[:, :, :], v_a[:, :, 0:VD], weight_a[:].unsqueeze(2).to_broadcast([P, HEADS, VD]), ALU.mult)\
                .then_inc(s["mixed"], 1)

        def dve_unit_rsum(dve, layer, s, u):
            w = (VD if u.kind == "a" else XD) + 1
            dve.wait_ge(s["values"], turns(layer, u))
            nc.vector.reciprocal(rsum[:, u.par, :].unsqueeze(2),
                                 value_ps[u.par][:, 0:GROUP * w].rearrange("p (h d) -> p h d", h=GROUP)[:, :, w - 1:w])\
                .then_inc(s["rsum"], 1)

        def dve_unit_divide(dve, layer, s, u):
            w, mix = (VD, mix_a) if u.kind == "a" else (XD, mix_x)
            if u.kind == "a" and u.group == 0 and static(u.batch) and u.batch == 1:
                dve.wait_ge(s["mixt_a"], 1)
            dve.wait_ge(s["rsum"], turns(layer, u))
            hs = heads_of(layer, u)
            nc.vector.tensor_tensor(mix[:, hs.start:hs[-1] + 1:hs.step, :],
                                    value_ps[u.par][:, 0:GROUP * (w + 1)].rearrange("p (h d) -> p h d", h=GROUP)[:, :, 0:w],
                                    rsum[:, u.par, :].unsqueeze(2).to_broadcast([P, GROUP, w]), ALU.mult)\
                .then_inc(s["divided"], 1)

        def dve_stats(dve, stats_done, kind, src, k):
            nc.vector.bn_stats(bns[kind][:], src).then_inc(stats_done, 1)
            hold(dve, stats_done, k + 1)
            return nc.vector.bn_aggr(mv[kind][:], bns[kind][:])

        def dve_stable(dve, stats_done, kind, src, k):
            nc.vector.tensor_reduce(rmax[kind][:], src, axis=AX_X, op=ALU.max)
            nc.vector.bn_stats(bns[kind][:], src).then_inc(stats_done, 1)
            hold(dve, stats_done, k + 1)
            nc.vector.reciprocal(rinv[kind][:], rmax[kind][:])
            return nc.vector.bn_aggr(mv[kind][:], bns[kind][:])

        def dve_job(dve, layer, s, j):
            cfg, ps, name, k = LAYERS[layer], job_ps[j.par], j.name, j.batch
            if name[0:2] not in ("qa", "va", "qx", "vx", "ya", "yx"):
                return
            dve.wait_ge(s["job"], j.count())
            blocks = ps[:, :].rearrange("p (n t) -> p n t", n=4)
            if name[0:2] == "qa":
                n = int(name[2])
                nc.vector.tensor_tensor(q_a[:, 4 * n:4 * n + 4, :], blocks,
                                        wa(layer, "bq")[:, 4 * n:4 * n + 4].unsqueeze(2).to_broadcast([P, 4, TOKENS]), ALU.add)\
                    .then_inc(s["q_a"], 1)
            elif name == "va":
                if cfg["own_values"] and (not static(k) or k > 0):
                    dve.wait_ge(s["mixed"], k)
                nc.vector.tensor_tensor(v_a[:, :, 0:VD], ps[:, 0:D].rearrange("p (h d) -> p h d", h=HEADS),
                                        wa(layer, "bv").rearrange("p (h d) -> p h d", h=HEADS), ALU.add)\
                    .then_inc(s["v_a"], 1)
            elif name[0:2] == "qx":
                n = int(name[2])
                nc.vector.tensor_copy(q_x[:, 4 * n:4 * n + 4, :], blocks)\
                    .then_inc(s["q_x"], 1)
            elif name[0:2] == "vx":
                n = int(name[2])
                nc.vector.tensor_copy(v_x[0:CTX, 8 * n:8 * n + 8, 0:XD], ps[0:CTX, :].rearrange("p (h d) -> p h d", h=8))\
                    .then_inc(s["v_x"], 1)
            elif name == "ya":
                dve.wait_ge(s["biased"], k + 1)
                nc.vector.tensor_tensor(y["a"][:], ps[:, 0:D], xres[:, bass.ds(k, 1), :].rearrange("p b d -> p (b d)"), ALU.add)\
                    .then_inc(s["y_a"], 1)
                dve.wait_ge(s["y_a"], k + 1)
                dve_stats(dve, s["st_a"], "a", y["a"][:], k).then_inc(s["mv_a"], 1)
                if cfg["stable"]:
                    dve.wait_ge(s["ya2"], k + 1)
                    dve_stable(dve, s["st_s"], "s", normed[:], k).then_inc(s["mv_s"], 1)
            elif cfg["stable"]:
                if static(k) and k == BATCHES - 1:
                    dve.wait_ge(s["normed_x"], k)
                nc.vector.tensor_copy(y["x"][:], ps[:, 0:D]).then_inc(s["y_x"], 1)
                dve.wait_ge(s["y_x"], k * 2 + 1)
                dve_stable(dve, s["st_z"], "z", y["x"][:], k).then_inc(s["mv_z"], 1)
                dve.wait_ge(s["y_x"], k * 2 + 2)
                dve_stats(dve, s["st_x"], "x", y["x"][:], k).then_inc(s["mv_x"], 1)
            else:
                if static(k) and k == BATCHES - 1:
                    dve.wait_ge(s["normed_x"], k)
                nc.vector.tensor_tensor(y["x"][:], ps[:, 0:D], xres[:, bass.ds(k, 1), :].rearrange("p b d -> p (b d)"), ALU.add)\
                    .then_inc(s["y_x"], 1)
                dve.wait_ge(s["y_x"], k + 1)
                dve_stats(dve, s["st_x"], "x", y["x"][:], k).then_inc(s["mv_x"], 1)

        def dve_slot(dve, layer, s, scored, flipped, valued, jobs):
            if scored:
                dve_unit_max(dve, layer, s, scored)
            if valued and mixes(layer, valued):
                dve_unit_rsum(dve, layer, s, valued)
            if flipped and not mixes(layer, flipped):
                dve_unit_sum(dve, layer, s, flipped)
                if flipped.group == GROUPS - 1:
                    dve_own_values(dve, s, flipped)
            elif flipped and flipped.par == 0:
                dve_unit_flip_out(dve, layer, s, flipped)
            if valued and mixes(layer, valued):
                dve_unit_divide(dve, layer, s, valued)
            for j in jobs:
                dve_job(dve, layer, s, j)

        def dve_layer(dve, layer):
            s = sig[layer]
            dve.wait_ge(in_attn[layer], 16)
            nb = LAYERS[layer]["blocks"]
            if LAYERS[layer]["stable"]:
                dve.wait_ge(in_cross[layer], 16)
                dve.sem_inc(s["flip_out_v"], CREDIT // 2)
                for semaphore in (s["rsum"], s["divided"], s["summed"]):
                    dve.sem_inc(semaphore, CREDIT)
                nc.vector.tensor_scalar(k_x[:, :, CTX:CTX + 1], wx(layer, "null").unsqueeze(1).to_broadcast([P, 8, 1]), X_SCALE,
                                        None, ALU.mult)
            nc.vector.tensor_scalar(kb_scaled[:, 0:nb], wa(layer, "bk"), LAYERS[layer]["scale"], None, ALU.mult)\
                .then_inc(ready_kb, 1)
            for slot in slots_before(layer):
                dve_slot(dve, layer, s, *slot)
            with dve.Fori(0, LOOPS) as b:
                for slot in slots_loop(layer, b):
                    dve_slot(dve, layer, s, *slot)
            for slot in slots_after(layer):
                dve_slot(dve, layer, s, *slot)

        def dve_experts(dve):
            count = [0]

            def step(ins):
                count[0] += 1
                ins.then_inc(moe["chain"], 1)
                dve.wait_ge(moe["chain"], count[0])

            def wide(t):
                return t[:].unsqueeze(2).to_broadcast([P, BATCHES, EXPERTS])

            logits = value_ps[0][:, 0:BATCHES * EXPERTS].rearrange("p (b e) -> p b e", b=BATCHES)
            rev = cut(const_sb, C_COLS, "rev8").rearrange("p (b e) -> p b e", b=BATCHES)
            nc.vector.tensor_copy(tri_b[:], cut(const_sb, C_COLS, "tri"))
            dve.wait_ge(moe["logits"], 1)
            step(nc.vector.tensor_reduce(tok["max"][:], logits, axis=AX_X, op=ALU.max))
            nc.vector.tensor_tensor(lg["centred"][:], logits, wide(tok["max"]), ALU.subtract).then_inc(moe["centred"], 1)
            dve.wait_ge(moe["centred"], 1)
            step(nc.vector.scalar_tensor_tensor(lg["pick"][:], lg["centred"][:], 0.0, rev, ALU.is_ge, ALU.mult))
            step(nc.vector.tensor_reduce(tok["pick"][:], lg["pick"][:], axis=AX_X, op=ALU.max))
            step(nc.vector.tensor_tensor(lg["onehot"][:], lg["pick"][:], wide(tok["pick"]), ALU.is_equal))
            nc.vector.tensor_copy(onehot_b[:], lg["onehot"][:]).then_inc(moe["onehot"], 1)
            dve.wait_ge(moe["exp"], 1)
            step(nc.vector.tensor_reduce(tok["sum"][:], lg["exp"][:], axis=AX_X, op=ALU.add))
            step(nc.vector.reciprocal(tok["prob"][:], tok["sum"][:]))
            step(nc.vector.tensor_scalar(tok["base"][:], tok["pick"][:], -float(CAP), float(CAP * EXPERTS - 1), ALU.mult, ALU.add))
            dve.wait_ge(moe["cum"], 1)
            cum = value_ps[1][:, 0:BATCHES * EXPERTS].rearrange("p (b e) -> p b e", b=BATCHES)
            step(nc.vector.tensor_tensor(lg["at"][:], cum, lg["onehot"][:], ALU.mult))
            step(nc.vector.tensor_reduce(tok["pos"][:], lg["at"][:], axis=AX_X, op=ALU.add))
            step(nc.vector.tensor_scalar(tok["kept"][:], tok["pos"][:], CAP + 0.5, None, ALU.is_le))
            step(nc.vector.scalar_tensor_tensor(tok["slot"][:], tok["pos"][:], float(CAP), tok["base"][:], ALU.min, ALU.add))
            step(nc.vector.tensor_scalar(tok["lost"][:], tok["kept"][:], -1.0, 1.0, ALU.mult, ALU.add))
            step(nc.vector.tensor_tensor(tok["spare"][:], cut(const_sb, C_COLS, "token"), tok["lost"][:], ALU.mult))
            step(nc.vector.tensor_tensor(tok["apart"][:], tok["slot"][:], tok["kept"][:], ALU.mult))
            step(nc.vector.tensor_tensor(tok["put"][:], tok["apart"][:], tok["spare"][:], ALU.add))
            nc.vector.tensor_copy(get_at[:], tok["slot"][:])
            nc.vector.tensor_copy(put_at[:], tok["put"][:]).then_inc(moe["put"], 1)
            step(nc.vector.tensor_tensor(tok["factor"][:], tok["kept"][:], tok["prob"][:], ALU.mult))
            step(nc.vector.tensor_scalar(tok["own"][:], tok["lost"][:], 1.0, None, ALU.add))
            for i in range(BATCHES):
                last = nc.vector.tensor_scalar(own[:, i, :], xres[:, i, :], tok["own"][:, i:i + 1], None, ALU.mult)
            last.then_inc(moe["own"], 1)

            def relu(e):
                dve.wait_ge(moe["up"], e * 2 + 2)
                if not static(e) or e > 0:
                    dve.wait_ge(moe["down"], e)
                nc.vector.tensor_scalar(hidden[:, 2:4, :], score_ps[1][:, 0:2 * CAP].rearrange("p (n t) -> p n t", n=2), 0.0, None,
                                        ALU.max).then_inc(moe["relu_v"], 1)

            def out_copy(i, e, par):
                dve.wait_ge(moe["down"], e + 1)
                if not static(i) or i > 0:
                    dve.wait_ge(moe["stored1"] if par else moe["stored0"], i * 16)
                nc.vector.tensor_copy(slot_out[:, par, :, :], value_ps[par][0:HALF, 0:2 * D].rearrange("p (t d) -> p t d", t=2))\
                    .then_inc(moe["out_sb"], 1)

            relu(0)
            out_copy(0, 0, 0)
            relu(1)
            out_copy(0, 1, 1)
            with dve.Fori(1, EXPERTS // 2) as i:
                relu(i * 2)
                out_copy(i, i * 2, 0)
                relu(i * 2 + 1)
                out_copy(i, i * 2 + 1, 1)
            dve.wait_ge(moe["own"], 1)
            dve.wait_ge(moe["gathered"], 16 * BATCHES)
            for i in range(BATCHES):
                step(nc.vector.scalar_tensor_tensor(y8[:, i, :], back[:, i, :], tok["factor"][:, i:i + 1], own[:, i, :], ALU.mult, ALU.add))
                step(nc.vector.bn_stats(bns8[:, i, :], y8[:, i, :]))
                last = nc.vector.bn_aggr(mv8[:, i, :], bns8[:, i, :])
            last.then_inc(moe["mv"], 1)
            dve.wait_ge(moe["rstd"], 1)
            for i in range(BATCHES):
                nc.vector.tensor_scalar(xres[:, i, :], y8[:, i, :], mv8[:, i, 0:1], rstd8[:, i:i + 1], ALU.subtract, ALU.mult)\
                    .then_inc(moe["done"], 1)

        def tile_of(k):
            return xres[:, bass.ds(k, 1), :].rearrange("p b d -> p (b d)")

        def dve_ffn(dve):
            rev = cut(const_sb, C_COLS, "rev16")
            N_ROUTE = 13

            def gates(k):
                dve.wait_ge(f["gate"], k + 1)
                nc.vector.tensor_copy(gate_sb[:], job_ps[0][:, 0:E2 + 2 * M2]).then_inc(f["gate_sb"], 1)

            def route(k):
                done = [0]

                def step(ins):
                    done[0] += 1
                    ins.then_inc(f["chain"], 1)
                    dve.wait_ge(f["chain"], k * N_ROUTE + done[0])

                def first_best(best, place, from_, key):
                    step(nc.vector.tensor_reduce(r1[best][:], from_, axis=AX_X, op=ALU.max))
                    step(nc.vector.scalar_tensor_tensor(r16[key][:], from_, r1[best][:], rev, ALU.is_equal, ALU.mult))
                    step(nc.vector.tensor_reduce(r1[place][:], r16[key][:], axis=AX_X, op=ALU.max))

                dve.wait_ge(f["exp"], k + 1)
                step(nc.vector.tensor_scalar(r16["sum"][:], r16["exp"][:], 1.0, None, ALU.add))
                step(nc.vector.reciprocal(r16["score"][:], r16["sum"][:]))
                first_best("m1", "x1", r16["score"][:], "w1")
                step(nc.vector.tensor_scalar(r16["one1"][:], r16["w1"][:], r1["x1"][:], None, ALU.is_equal))
                step(nc.vector.scalar_tensor_tensor(r16["rest"][:], r16["one1"][:], -4.0, r16["score"][:], ALU.mult, ALU.add))
                first_best("m2", "x2", r16["rest"][:], "w2")
                step(nc.vector.tensor_scalar(r16["two"][:], r16["w2"][:], r1["x2"][:], r1["m2"][:], ALU.is_equal, ALU.mult))
                step(nc.vector.tensor_scalar(r1["sum"][:], r1["m1"][:], r1["m2"][:], 1e-20, ALU.add, ALU.add))
                step(nc.vector.reciprocal(r1["inv"][:], r1["sum"][:]))
                nc.vector.scalar_tensor_tensor(r16["sum"][:], r16["one1"][:], r1["m1"][:], r16["two"][:], ALU.mult, ALU.add)\
                    .then_inc(f["w"], 1)
                assert done[0] == N_ROUTE
                dve.wait_ge(f["w"], k * 4 + 1)
                if not static(k) or k > 0:
                    dve.wait_ge(f["routed"], k * 2)
                nc.vector.tensor_scalar(r16["route"][:], r16["sum"][:], r1["inv"][:], 0.5 * ROUTE_SCALE, ALU.mult, ALU.mult)\
                    .then_inc(f["route"], 1)

            def silus(k):
                dve.wait_ge(f["tanh_s"], k + 1)
                nc.vector.scalar_tensor_tensor(hid_s[:], tanh_s[:], 1.0, gate_sb[:, E2:E2 + M2], ALU.add, ALU.mult).then_inc(f["w"], 1)
                dve.wait_ge(f["w"], k * 4 + 2)
                if not static(k) or k > 0:
                    dve.wait_ge(f["flip_s"], k)
                nc.vector.scalar_tensor_tensor(hid_s2[:], hid_s[:], 0.5, gate_sb[:, E2 + M2:], ALU.mult, ALU.mult)\
                    .then_inc(f["hid_s"], 1)
                for c in range(2):
                    dve.wait_ge(f["tanh"], k * 2 + (1 + c))
                    nc.vector.scalar_tensor_tensor(tanh_g[:, c, :], tanh_g[:, c, :], 1.0, up_ps[c][0][:, :], ALU.add, ALU.mult)\
                        .then_inc(f["w"], 1)
                    dve.wait_ge(f["w"], k * 4 + (3 + c))
                    nc.vector.tensor_tensor(hid[:, c, :], tanh_g[:, c, :], up_ps[c][1][:, :], ALU.mult).then_inc(f["hid"], 1)

            def end(k):
                dve.wait_ge(f["down"], k + 1)
                if not static(k) or k > 0:
                    dve.wait_ge(f["normed"], k)
                nc.vector.tensor_tensor(y_f[:], job_ps[1][:, 0:D], tile_of(k), ALU.add).then_inc(f["y"], 1)
                dve.wait_ge(f["y"], k + 1)
                nc.vector.bn_stats(bns["x"][:], y_f[:]).then_inc(f["st"], 1)
                hold(dve, f["st"], k + 1)
                nc.vector.bn_aggr(mv["x"][:], bns["x"][:]).then_inc(f["mv"], 1)

            def front(k):
                gates(k)
                route(k)
                silus(k)

            front(0)
            front(1)
            end(0)
            with dve.Fori(2, BATCHES) as k:
                front(k)
                end(k - 1)
            end(BATCHES - 1)

        def steps_of(gp, semaphore, k, n):
            done = [0]

            def step(ins):
                done[0] += 1
                assert done[0] <= n
                ins.then_inc(semaphore, 1)
                hold(gp, semaphore, k * n + done[0])
            return step

        def gp_scale(gp, step, var):
            step(gp.tensor_scalar(ve[:], var, LN_EPS, None, ALU.add))
            step(gp.tensor_tensor(rstd[:], ve[:], minus_half[:], ALU.pow))

        def gp_norm(gp, step, dst, kind, src):
            gp_scale(gp, step, mv[kind][:, 1:2])
            return gp.tensor_scalar(dst, src, mv[kind][:, 0:1], rstd[:], ALU.subtract, ALU.mult)

        def gp_stable_norm(gp, step, dst, kind, src):
            r = rinv[kind][:]
            step(gp.tensor_scalar(r2[:], mv[kind][:, 1:2], r, r, ALU.mult, ALU.mult))
            gp_scale(gp, step, r2[:])
            step(gp.tensor_tensor(rstd_r[:], rstd[:], r, ALU.mult))
            return gp.tensor_scalar(dst, src, mv[kind][:, 0:1], rstd_r[:], ALU.subtract, ALU.mult)

        def gp_take(gp, layer, s, k):
            if not static(k) or k > 0:
                hold(gp, s["xt_a"], k)
            gp.tensor_copy(cur_a[:], tile_of(k)).then_inc(s["cur_a"], 1)
            hold(gp, s["cur_a"], k + 1)
            gp.tensor_tensor(tile_of(k), tile_of(k), wa(layer, "bo"), ALU.add).then_inc(s["biased"], 1)

        def gp_after_a(gp, layer, s, k):
            hold(gp, s["mv_a"], k + 1)
            if LAYERS[layer]["stable"]:
                step = steps_of(gp, s["gp_a"], k, 6)
                gp_norm(gp, step, normed[:], "a", y["a"][:]).then_inc(s["ya2"], 1)
                hold(gp, s["ya2"], k + 1)
                gp.tensor_copy(tile_of(k), normed[:])
                hold(gp, s["mv_s"], k + 1)
                if not static(k) or k > 0:
                    hold(gp, s["xt_x"], k)
                gp_stable_norm(gp, step, cur_x[:], "s", normed[:]).then_inc(s["cur_x"], 1)
            else:
                step = steps_of(gp, s["gp_a"], k, 2)
                if not static(k) or k > 0:
                    hold(gp, s["xt_x"], k)
                gp_norm(gp, step, cur_x[:], "a", y["a"][:]).then_inc(s["cur_x"], 1)
                hold(gp, s["cur_x"], k + 1)
                gp.tensor_tensor(tile_of(k), cur_x[:], wx(layer, "row"), ALU.add)

        def gp_after_x(gp, layer, s, k):
            if LAYERS[layer]["stable"]:
                step = steps_of(gp, s["gp_x"], k, 8)
                hold(gp, s["mv_z"], k + 1)
                gp_stable_norm(gp, step, z[:], "z", y["x"][:]).then_inc(s["gp_z"], 1)
                hold(gp, s["gp_z"], k + 1)
                step(gp.tensor_tensor(z[:], z[:], wx(layer, "row"), ALU.mult))
                gp.tensor_tensor(y["x"][:], z[:], tile_of(k), ALU.add).then_inc(s["y_x"], 1)
            else:
                step = steps_of(gp, s["gp_x"], k, 3)
            hold(gp, s["mv_x"], k + 1)
            step(gp_norm(gp, step, normed[:], "x", y["x"][:]))
            gp.tensor_copy(tile_of(k), normed[:]).then_inc(s["normed_x"], 1)

        def gp_layer(gp, layer):
            s = sig[layer]
            gp.wait_ge(in_attn[layer], 16)
            gp.wait_ge(in_cross[layer], 16)
            gp.wait_ge(ready_ones, 1)
            gp_take(gp, layer, s, 0)
            gp_take(gp, layer, s, 1)
            gp_after_a(gp, layer, s, 0)
            with gp.Fori(0, LOOPS) as b:
                gp_take(gp, layer, s, b + 2)
                gp_after_a(gp, layer, s, b + 1)
                gp_after_x(gp, layer, s, b)
            gp_after_a(gp, layer, s, 7)
            gp_after_x(gp, layer, s, 6)
            gp_after_x(gp, layer, s, 7)

        def gp_experts(gp):
            gp.wait_ge(sig[0]["normed_x"], BATCHES)
            gp.memset(ones_b[:], 1.0).then_inc(moe["ready"], 1)
            gp.wait_ge(moe["put"], 1)
            gp.wait_ge(moe["cleared"], 16)
            for i in range(BATCHES):
                gp.indirect_dma_start(out=slots_dram[:, :], out_offset=bass.IndirectOffsetOnAxis(ap=put_at[:, i:i + 1], axis=0),
                                      in_=xres[:, i, :], in_offset=None).then_inc(moe["scattered"], 16)
            gp.wait_ge(moe["stored0"], 8 * EXPERTS)
            gp.wait_ge(moe["stored1"], 8 * EXPERTS)
            for i in range(BATCHES):
                gp.indirect_dma_start(out=back[:, i, :], out_offset=None, in_=outs_dram[:, :],
                                      in_offset=bass.IndirectOffsetOnAxis(ap=get_at[:, i:i + 1], axis=0)).then_inc(moe["gathered"], 16)
            gp.wait_ge(moe["mv"], 1)
            gp.tensor_scalar(ve8[:], mv8[:, :, 1], LN_EPS, None, ALU.add).then_inc(moe["gp"], 1)
            gp.wait_ge(moe["gp"], 1)
            gp.tensor_tensor(rstd8[:], ve8[:], half8[:], ALU.pow).then_inc(moe["rstd"], 1)
            gp.wait_ge(moe["done"], BATCHES)

        def gp_ffn(gp):
            def take(k):
                if not static(k) or k > 0:
                    hold(gp, f["turned"], k)
                gp.tensor_copy(cur_a[:], tile_of(k)).then_inc(f["cur"], 1)

            def routes(k):
                hold(gp, f["route"], k + 1)
                n = BANK // M2
                for c in range(2):
                    if not static(k) or k > 0:
                        hold(gp, f["flip1"] if c else f["flip0"], k)
                    hold(gp, f["hid"], k * 2 + (1 + c))
                    gp.tensor_tensor(hid_r[:, c, :].rearrange("p (e m) -> p e m", e=n), hid[:, c, :].rearrange("p (e m) -> p e m", e=n),
                                     r16["route"][:, c * n:(c + 1) * n].unsqueeze(2).to_broadcast([P, n, M2]), ALU.mult)\
                        .then_inc(f["routed"], 1)

            def norm(k):
                hold(gp, f["mv"], k + 1)
                step = steps_of(gp, f["gp"], k, 2)
                gp_scale(gp, step, mv["x"][:, 1:2])
                if not static(k) or k > 0:
                    hold(gp, f["out"], k * 16)
                gp.tensor_scalar(out_sb[:], y_f[:], mv["x"][:, 0:1], rstd[:], ALU.subtract, ALU.mult).then_inc(f["normed"], 1)

            gp.wait_ge(in_ffn, 16)
            take(0)
            take(1)
            routes(0)
            take(2)
            routes(1)
            norm(0)
            with gp.Fori(2, BATCHES - 1) as k:
                take(k + 1)
                routes(k)
                norm(k - 1)
            routes(BATCHES - 1)
            norm(BATCHES - 2)
            norm(BATCHES - 1)

        def sp_layer(sp, layer):
            s = sig[layer]
            if layer:
                sp.wait_ge(sig[0]["job"], BATCHES * PER_LOOP[0])
            sp.dma_start(ctx_cur[:], ctx_t[:, 0:1, :].rearrange("p b c -> p (b c)")).then_inc(s["ctx"], 16)
            with sp.Fori(1, BATCHES) as k:
                sp.wait_ge(s["v_x"], k * 2)
                sp.dma_start(ctx_cur[:], ctx_t[:, bass.ds(k, 1), :].rearrange("p b c -> p (b c)")).then_inc(s["ctx"], 16)

        def sp_experts(sp):
            def weights(e, par):
                w_in = moe["w_in1"] if par else moe["w_in0"]
                sp.dma_start(w1_sb[:, par:par + 1, :], w1[bass.ds(e, 1), :, :].rearrange("e d f -> d e f")).then_inc(w_in, 16)
                sp.dma_start(w2_sb[:, par, :, :], w2[bass.ds(e, 1), :, :].rearrange("e (b f) d -> f (e b) d", f=P)).then_inc(w_in, 16)

            def slots(e, par):
                sp.dma_start(slot_in[:, par, :, :], slots_dram[bass.ds(e * CAP, CAP), :].rearrange("(t p) d -> p t d", p=HALF))\
                    .then_inc(moe["slot_in1"] if par else moe["slot_in0"], 16)

            def store(e, par):
                sp.wait_ge(moe["out_sb"], e + 1)
                sp.dma_start(outs_dram[bass.ds(e * CAP, CAP), :].rearrange("(t p) d -> p t d", p=HALF), slot_out[:, par, :, :])\
                    .then_inc(moe["stored1"] if par else moe["stored0"], 16)

            weights(0, 0)
            weights(1, 1)
            sp.wait_ge(moe["scattered"], 16 * BATCHES)
            slots(0, 0)
            slots(1, 1)
            with sp.Fori(0, EXPERTS // 2 - 1) as i:
                for par in range(2):
                    sp.wait_ge(moe["down"], i * 2 + (1 + par))
                    weights(i * 2 + (2 + par), par)
                    slots(i * 2 + (2 + par), par)
                    store(i * 2 + par, par)
            store(EXPERTS - 2, 0)
            store(EXPERTS - 1, 1)

        def sp_ffn(sp):
            with sp.Fori(0, BATCHES) as k:
                sp.wait_ge(f["normed"], k + 1)
                sp.dma_start(out[bass.ds(k, 1), :, :].rearrange("b t d -> t (b d)"), out_sb[:]).then_inc(f["out"], 16)
            sp.wait_ge(f["out"], 16 * BATCHES)

        block = stack.enter_context(nc.Block())

        @block.sync
        def _(sp):
            sp.dma_start(attn_sb[0][:], attn[0]).then_inc(in_attn[0], 16)
            sp.dma_start(xres[:], x.rearrange("b t d -> t b d")).then_inc(in_x, 16)
            sp.dma_start(const_sb[:], consts).then_inc(in_const, 16)
            sp.dma_start(cross_sb[0][:], cross[0]).then_inc(in_cross[0], 16)
            sp.dma_start(attn_sb[1][:], attn[1]).then_inc(in_attn[1], 16)
            sp.dma_start(cross_sb[1][:], cross[1]).then_inc(in_cross[1], 16)
            sp.dma_start(v_x[CTX:CTX + 1, :, 0:XD], null_v).then_inc(in_null, 16)
            sp.dma_start(ffn_sb[:], ffn).then_inc(in_ffn, 16)
            sp.wait_ge(ready_ones, 1)
            sp.dma_start(slots_dram[0:SLOTS, :].rearrange("(p n) d -> p (n d)", p=P), zeros[:]).then_inc(moe["cleared"], 16)
            sp_layer(sp, 0)
            sp_experts(sp)
            sp_layer(sp, 1)
            sp_ffn(sp)

        @block.tensor
        def _(pe):
            pe_layer(pe, 0)
            pe_experts(pe)
            pe_layer(pe, 1)
            pe_ffn(pe)

        @block.scalar
        def _(act):
            act_layer(act, 0)
            act_experts(act)
            act_layer(act, 1)
            act_ffn(act)

        @block.vector
        def _(dve):
            dve_layer(dve, 0)
            dve_experts(dve)
            dve_layer(dve, 1)
            dve_ffn(dve)

        @block.gpsimd
        def _(gp):
            gp.memset(minus_half[:], -0.5)
            gp.memset(half8[:], -0.5)
            gp.memset(zeros[:], 0.0)
            gp.memset(v_a[:, :, VD:VD + 1], 1.0)
            gp.memset(v_x[:, :, XD:XD + 1], 1.0).then_inc(ready_ones, 1)
            gp.wait_ge(in_x, 16)
            gp_layer(gp, 0)
            gp_experts(gp)
            gp_layer(gp, 1)
            gp_ffn(gp)


def pad_heads(w, per_head, step, blocks):
    rows = w.shape[0]
    out = np.zeros((rows, HEADS, step), w.dtype)
    out[:, :, 0:per_head] = w
    return out.reshape(rows, blocks * P)


def lay_attn0(i):
    def both(w, r):
        return np.concatenate([r.reshape(-1, HEADS, 32), w.reshape(-1, HEADS, 8)], axis=2)

    wq, wk = (pad_heads(both(i[f"L0_attn_W{n}"], i["L0_attn_Wr"]), 40, 64, 8) for n in "qk")
    bq, bk = (pad_heads(both(i[f"L0_attn_b{n}"], i["L0_attn_br"]), 40, 64, 8).reshape(8, P).T for n in "qk")
    rows = [np.broadcast_to(i[f"L0_attn_b{n}"], (P, D)) for n in "vo"]
    return np.concatenate([wq, wk, i["L0_attn_Wv"], i["L0_attn_Wo"], *rows, bq, bk], axis=1)


def lay_attn1(i):
    w = i["L1_attn_w_in"].T.reshape(D, HEADS, 3, 8)
    bias = i["L1_attn_b_in"].reshape(1, HEADS, 3, 8)
    wq, wk = (pad_heads(w[:, :, n], 8, 32, 4) for n in range(2))
    bq, bk = (pad_heads(bias[:, :, n], 8, 32, 4).reshape(4, P).T for n in range(2))
    rows = [np.broadcast_to(bias[:, :, 2].reshape(D), (P, D)), np.broadcast_to(i["L1_attn_b_out"], (P, D))]
    return np.concatenate([wq, wk, w[:, :, 2].reshape(D, D), i["L1_attn_w_out"].T, *rows, bq, bk], axis=1)


def lay_cross(wq, wk, wv, wo, row, col, null_key):
    wo = wo.reshape(8, P, D).transpose(1, 0, 2).reshape(P, 8 * D)
    return np.concatenate([wq, wk, wv, wo, np.broadcast_to(row, (P, D)), col.reshape(P, 1),
                           np.tile(null_key, 2).reshape(P, 1)], axis=1)


def lay_ffn(i):
    def wide(w):
        return w.transpose(1, 0, 2).reshape(D, E2 * M2)

    down = np.zeros((9 * P, D), np.float32)
    down[0:E2 * M2] = i["L1_ffn_w_down"].reshape(E2 * M2, D)
    down[E2 * M2:GU] = i["L1_ffn_ws_down"]
    down = down.reshape(9, P, D).transpose(1, 0, 2).reshape(P, 9 * D)
    return np.concatenate([wide(i["L1_ffn_w_gate"]), wide(i["L1_ffn_w_up"]), i["L1_ffn_ws_gate"], i["L1_ffn_ws_up"],
                           down, i["L1_ffn_gate_w"].T], axis=1)


def lay_consts(wr):
    f = np.float32
    rows = [np.broadcast_to(np.tile(np.arange(EXPERTS, 0, -1, dtype=f), BATCHES), (P, BATCHES * EXPERTS)),
            np.broadcast_to(np.arange(E2, 0, -1, dtype=f), (P, E2))]
    token = SLOTS + np.arange(BATCHES, dtype=f)[None, :] * P + np.arange(P, dtype=f)[:, None]
    return np.concatenate([np.eye(P, dtype=f), *rows, token, wr, np.triu(np.ones((P, P), f))], axis=1)


def kernel(**inputs):
    import concourse.bacc as _bacc
    from concourse.bass_utils import run_bass_kernel_spmd as _run

    i = {k: np.asarray(v) for k, v in inputs.items()}
    wkv = i["L1_xattn_Wkv"]
    arrays = {
        "x": i["x"],
        "ctx_t": i["ctx_1024"].transpose(2, 0, 1),
        "consts": lay_consts(i["L0_ffn_Wr"]),
        "attn0": lay_attn0(i),
        "attn1": lay_attn1(i),
        "cross0": lay_cross(i["L0_xattn_Wq"], i["L0_xattn_Wk"], i["L0_xattn_Wv"], i["L0_xattn_Wo"], i["L0_xattn_bo"],
                            np.ones(P, np.float32), np.zeros(XD, np.float32)),
        "cross1": lay_cross(i["L1_xattn_Wq"], wkv[:, :1024], wkv[:, 1024:], i["L1_xattn_Wo"], i["L1_xattn_g_out"],
                            i["L1_xattn_g_in"], i["L1_xattn_null_kv"][0]),
        "null_v": np.broadcast_to(i["L1_xattn_null_kv"][1], (1, HEADS, XD)),
        "w1": i["L0_ffn_W1"],
        "w2": i["L0_ffn_W2"],
        "ffn": lay_ffn(i),
    }
    arrays = {k: np.ascontiguousarray(v) for k, v in arrays.items()}
    nc = _bacc.Bacc("TRN2", target_bir_lowering=False, num_devices=1)
    a = {n: nc.dram_tensor(n, v.shape, mybir.dt.from_np(v.dtype), kind="ExternalInput").ap() for n, v in arrays.items()}
    out = nc.dram_tensor("out", (BATCHES, TOKENS, D), F32, kind="ExternalOutput").ap()
    decoder(nc, a["x"], a["ctx_t"], a["consts"], (a["attn0"], a["attn1"]), (a["cross0"], a["cross1"]), a["null_v"], a["w1"], a["w2"], a["ffn"], out)
    r = _run(nc, [arrays], core_ids=[0])
    return r.results[0]["out"]
```

```python
from contextlib import ExitStack

import numpy as np

import concourse.bass as bass
from concourse import mybir

F32 = mybir.dt.float32
BF16 = mybir.dt.bfloat16
U32 = mybir.dt.uint32
ALU = mybir.AluOpType
ACT = mybir.ActivationFunctionType
AX_X = mybir.AxisListType.X

P = 128
BATCHES = 8
TOKENS = 128
D = 128
HEADS = 16
GROUP = 4
GROUPS = HEADS // GROUP
CTX = 77
HALF_CTX = BATCHES // 2 * CTX
XD = 64
VD = 8
LN_EPS = 1e-5
BANK = 512

EXPERTS = 8
CAP = int(1.25 * BATCHES * TOKENS / EXPERTS)
SLOTS = EXPERTS * CAP
ROUND = 4
ROUNDS = EXPERTS // ROUND
ROUND_TILES = ROUND * CAP // P
EARLY_VALUES = 4
NORM_GROUPS = (range(0, 2), range(2, 6), range(6, BATCHES))
FB = 4

E2 = 16
M2 = 64
ROUTE_SCALE = 2.5

LAYERS = (
    dict(blocks=8, rows=40, step=64, scale=1.0 / (8 + 32) ** 0.5, keys=CTX, stable=False, own_values=False),
    dict(blocks=4, rows=8, step=32, scale=1.0 / 8 ** 0.5, keys=CTX + 1, stable=True, own_values=True),
)
X_SCALE = XD ** -0.5


def columns(*parts):
    at, out = 0, {}
    for name, width in parts:
        out[name] = (at, at + width)
        at += width
    return out, at


def attn_columns(layer):
    n = LAYERS[layer]["blocks"]
    return columns(("wq", n * P), ("wk", n * P), ("wv", D), ("wo", D), ("bv", D), ("bo", D), ("bq", n), ("bk", n))


X_COLS = columns(("wq", 1024), ("wk", 1024), ("wv", 1024), ("wo", 1024), ("row", D), ("col", 1), ("null", 1))
GU = E2 * M2 + M2
F_COLS = columns(("wg", E2 * M2), ("wu", E2 * M2), ("ws", 2 * M2), ("wd", 9 * D), ("gate", E2))
C_COLS = columns(("ident", P), ("rev8", BATCHES * EXPERTS), ("rev16", E2), ("token", BATCHES), ("wr", EXPERTS),
                 ("tri", P))


class Unit:

    def __init__(self, kind, batch, group, b, c):
        self.kind, self.batch, self.group, self.b, self.c = kind, batch, group, b, c
        self.par = c % 2

    def count(self, back=0):
        return self.b * 8 + (self.c + 1 - back)

    def half(self):
        return self.b * 4 + (self.c // 2 + 1)


MIX_CREDIT = 2
CREDIT = 2


def turns(layer, u, back=0):
    if not LAYERS[layer]["own_values"]:
        return u.count(back)
    return u.batch * GROUPS + (u.group + 1 + CREDIT - back)


def half_turns(layer, u):
    if not LAYERS[layer]["own_values"]:
        return u.half()
    return u.batch * (GROUPS // 2) + (u.group // 2 + 1 + CREDIT // 2)


def has_turned(layer, u):
    return LAYERS[layer]["own_values"] or not isinstance(u.b, int) or u.c >= 2


def heads_of(layer, u):
    per = P // LAYERS[layer]["step"] if u.kind == "a" else P // XD
    first = u.group % per + per * GROUP * (u.group // per)
    return range(first, first + per * GROUP, per)


class Job:

    def __init__(self, name, batch, b=0, c=0, per=0, before=None):
        self.name, self.batch, self.b, self.c, self.per, self.before = name, batch, b, c, per, before
        self.par = c % 2

    def count(self):
        return self.b * self.per + (self.c + 1)




def job_names(layer):
    n = LAYERS[layer]["blocks"] // 4
    qa = [f"qa{i}" for i in range(n)]
    ka = [f"ka{i}" for i in range(n)]
    return qa, ka, ["qx0", "qx1"], ["tx0", "tx1"]


KEY_JOBS = [f"kc{i}" for i in range(16)]
VALUE_JOBS = [f"vc{i}" for i in range(16)]


def before_loop(layer):
    qa, ka, qx, tx = job_names(layer)
    if layer:
        return [[("xa", 0)] + [(n, 0) for n in qa + ka] + [("va", 0)],
                [("xa", 1)], [], [], [(n, 1) for n in qa], [(n, 1) for n in ka], [("ta", 0), ("va", 1)],
                [("ya", 0)], [("sa", 0)], [], [("xx", 0)] + [(n, 0) for n in qx]]
    c = [(n, 0) for n in KEY_JOBS + VALUE_JOBS]
    return [[("xa", 0)] + [(n, 0) for n in qa + ka] + [("va", 0)],
            c[0:4], c[4:8], c[8:12] + [("xa", 1)], [(n, 1) for n in qa + ka],
            c[12:14], c[14:16], c[16:18] + [("va", 1)],
            [("ta", 0)] + c[18:20] + [("ya", 0), ("sa", 0)] + c[20:29] + [("xx", 0)] + c[29:32] + [(n, 0) for n in qx]]


def in_loop(layer):
    qa, ka, qx, tx = job_names(layer)
    if layer:
        return [[("xa", 2), ("yx", 0), ("sz", 0)], [(n, 2) for n in qa + ka], [("ta", 1), ("sx", 0)], [("va", 2), ("ya", 1)],
                [("sa", 1)], [], [], [("xx", 1), ("tx0", 0), ("qx0", 1), ("qx1", 1), ("tx1", 0)]]
    return [[("xa", 2)], [(n, 2) for n in qa], [(n, 2) for n in ka], [("ta", 1), ("va", 2)],
            [("ya", 1)], [("tx0", 0)], [("xx", 1)], [("tx1", 0), ("qx0", 1), ("qx1", 1), ("yx", 0)]]


def after_loop(layer):
    if layer:
        return [[("yx", 6)], [("ta", 7), ("sz", 6)], [("ya", 7)], [("sx", 6)], [("tx0", 6), ("sa", 7)],
                [("xx", 7), ("qx0", 7), ("qx1", 7)],
                [], [("tx1", 6)], [("yx", 7), ("sz", 7)], [], [("sx", 7)], [("tx0", 7)], [("tx1", 7), ("yx", 8), ("sz", 8)]]
    return [[], [], [], [("ta", 7), ("ya", 7)], [("tx0", 6)], [("sa", 7), ("xx", 7), ("qx0", 7), ("qx1", 7)],
            [], [("tx1", 6), ("yx", 6)], [], [], [], [("tx0", 7)], [("tx1", 7), ("yx", 7)]]


NOT_JOBS = ("sa", "sz", "sx")
EARLY_JOBS = ("qa0", "qa1")


def job_count(slots):
    return sum(name not in NOT_JOBS for slot in slots for name, k in slot)


PER_LOOP = [job_count(in_loop(layer)) for layer in range(2)]
LOOPS = BATCHES - 2


def numbered(layer, slots, first, b, before):
    out, made = [], list(before)
    for slot in slots:
        out.append([])
        for name, k in slot:
            if name in NOT_JOBS:
                out[-1].append(Job(name, b + k))
                continue
            made.append(Job(name, b + k, b, first + len(made) - 2, PER_LOOP[layer], made[-2]))
            out[-1].append(made[-1])
    return out


def last_two(layer, b):
    return [Job("qx1", b), Job("tx1", b - 1)] if layer else [Job("qx1", b), Job("yx", b - 1)]


def slots_before(layer):
    units = [Unit("a", 0, g, 0, g) for g in range(GROUPS)]
    units += [None] * (2 if layer else 0)
    units += [Unit("a", 1, g, 0, 4 + g) for g in range(GROUPS)]
    jobs = numbered(layer, before_loop(layer), 0, 0, [None, None])
    return [(None, None, None, jobs[0])] + [
        (u, units[i - 2] if i >= 2 else None, units[i - 3] if i >= 3 else None, jobs[i + 1])
        for i, u in enumerate(units)]


def slots_loop(layer, b):
    first = job_count(before_loop(layer))
    units = [Unit("a", b + 1, g, b, 4 + g) for g in range(1, GROUPS)]
    units += [Unit("x", b, g, b, 8 + g) for g in range(GROUPS)] + [Unit("a", b + 2, g, b, 12 + g) for g in range(GROUPS)]
    plan = numbered(layer, in_loop(layer), first, b, last_two(layer, b))
    return [(units[i + 3], units[i + 1], units[i], jobs) for i, jobs in enumerate(plan)]


def slots_after(layer):
    first = job_count(before_loop(layer)) + LOOPS * PER_LOOP[layer]
    n = 8 * (BATCHES - 1)
    units = [Unit("a", 7, g, 0, n - 4 + g) for g in range(1, GROUPS)]
    units += [Unit("x", 6, g, 0, n + g) for g in range(GROUPS)] + [None] * 2
    units += [Unit("x", 7, g, 0, n + 4 + g) for g in range(GROUPS)] + [None] * 3
    plan = numbered(layer, after_loop(layer), first, 0, last_two(layer, LOOPS))
    return [(units[i + 3], units[i + 1], units[i], jobs) for i, jobs in enumerate(plan)]


def decoder(nc, x, ctx_t, consts, attn, cross, null_v, w1, w2, ffn, out):
    stack = ExitStack()
    with stack:
        def sb(name, shape, dt=F32):
            return stack.enter_context(nc.sbuf_tensor(name, shape, dt))

        def sem(name):
            return stack.enter_context(nc.semaphore(name))

        const_sb = sb("const_sb", [P, C_COLS[1]])
        attn_sb = [sb(f"attn_sb{n}", [P, attn_columns(n)[1]]) for n in range(2)]
        cross_sb = [sb(f"cross_sb{n}", [P, X_COLS[1]]) for n in range(2)]
        ffn_sb = sb("ffn_sb", [P, F_COLS[1]])

        def cut(tensor, table, name):
            a, b = table[0][name]
            return tensor[:, a:b]

        ident = cut(const_sb, C_COLS, "ident")

        def wa(layer, name):
            return cut(attn_sb[layer], attn_columns(layer), name)

        def wx(layer, name):
            return cut(cross_sb[layer], X_COLS, name)

        xres = sb("xres", [P, BATCHES, D])
        cur_a = sb("cur_a", [P, D])
        cur_x = sb("cur_x", [P, D])
        ctx_all = sb("ctx_all", [P, BATCHES * CTX])
        xt_a = sb("xt_a", [P, TOKENS])
        xt_x = sb("xt_x", [P, TOKENS])
        q_a = sb("q_a", [P, 8, TOKENS])
        k_a = sb("k_a", [P, 8, TOKENS])
        v_a = sb("v_a", [P, HEADS, VD + 1])
        q_x = sb("q_x", [P, 8, TOKENS])
        k_x = sb("k_x", [P, BATCHES, 8, CTX + 1])
        k_cur = sb("k_cur", [P, 8, CTX + 1])
        v_x = sb("v_x", [CTX + 1, BATCHES, HEADS, XD + 1])
        negmax = sb("negmax", [P, 2, GROUP])
        probs = sb("probs", [P, 2, GROUP, TOKENS])
        probs_t = sb("probs_t", [P, 2, GROUP, TOKENS])
        rsum = sb("rsum", [P, 2, GROUP])
        probs_a = sb("probs_a", [P, 2, GROUP, TOKENS])
        sums_a = sb("sums_a", [P, HEADS])
        inv_a = sb("inv_a", [P, HEADS])
        weight_a = sb("weight_a", [P, HEADS])
        mix_a = sb("mix_a", [P, HEADS, VD])
        mix_x = sb("mix_x", [P, HEADS, XD])
        mixt_a = sb("mixt_a", [P, TOKENS])
        mixt_x = sb("mixt_x", [P, 8, TOKENS])
        kb_scaled = sb("kb_scaled", [P, 8])
        y = {k: sb(f"y_{k}", [P, D]) for k in "ax"}
        bns = {k: sb(f"bns_{k}", [P, 6]) for k in "axsz"}
        mv = {k: sb(f"mv_{k}", [P, 2]) for k in "axsz"}
        rmax = {k: sb(f"rmax_{k}", [P, 1]) for k in "sz"}
        rinv = {k: sb(f"rinv_{k}", [P, 1]) for k in "sz"}
        ve = sb("ve", [P, 1])
        rstd = sb("rstd", [P, 1])
        r2 = sb("r2", [P, 1])
        rstd_r = sb("rstd_r", [P, 1])
        z = sb("z", [P, D])
        minus_half = sb("minus_half", [P, 1])
        normed = sb("normed", [P, D])

        x2t, back, y8, own = q_a, k_a, q_x, mixt_x
        lg = {n: sb(f"lg_{n}", [P, BATCHES, EXPERTS]) for n in ("centred", "exp", "pick", "onehot", "at")}
        onehot_b = sb("onehot_b", [P, BATCHES, EXPERTS], BF16)
        tri_b = sb("tri_b", [P, P], BF16)
        ones_b = sb("ones_b", [P, P], BF16)
        tok = {n: sb(f"tok_{n}", [P, BATCHES]) for n in ("max", "sum", "prob", "pick", "pos", "kept", "slot", "spare",
                                                           "apart", "put", "base", "lost", "own", "factor")}
        put_at = sb("put_at", [P, BATCHES], U32)
        get_at = sb("get_at", [P, BATCHES], U32)
        slot_in = sb("slot_in", [P, SLOTS // P, D])
        slot_t = sb("slot_t", [P, SLOTS])
        w1_sb = sb("w1_sb", [P, ROUND, FB * P])
        w2_sb = sb("w2_sb", [P, ROUND, FB, D])
        hidden = sb("hidden", [P, 2, FB, CAP])
        out_t = sb("out_t", [P, ROUND * CAP])
        slot_out = sb("slot_out", [P, ROUND_TILES, D])
        zeros = slot_t
        bns8 = sb("bns8", [P, BATCHES, 6])
        mv8 = sb("mv8", [P, BATCHES, 2])
        ve8 = sb("ve8", [P, BATCHES])
        rstd8 = sb("rstd8", [P, BATCHES])
        half8 = sb("half8", [P, BATCHES])
        slots_dram = nc.dram_tensor("slots_dram", (SLOTS + BATCHES * TOKENS, D), F32).ap()
        outs_dram = nc.dram_tensor("outs_dram", (SLOTS, D), F32).ap()

        xt_f = sb("xt_f", [P, TOKENS])
        gate_sb = sb("gate_sb", [P, E2 + 2 * M2])
        tanh_g = w1_sb[:, 0:2, :]
        hid = w1_sb[:, 2:4, :]
        hid_r = w2_sb[:, 0:2, :, :].rearrange("p a b d -> p a (b d)")
        tanh_s = sb("tanh_s", [P, M2])
        hid_s = sb("hid_s", [P, M2])
        hid_s2 = sb("hid_s2", [P, M2])
        ht = w2_sb[:, 2:4, :, :].rearrange("p a b d -> p (a b) d")
        ht_s = sb("ht_s", [M2, TOKENS])
        r16 = {n: sb(f"r16_{n}", [P, E2]) for n in ("exp", "score", "w1", "one1", "rest", "w2", "two", "sum", "route")}
        r1 = {n: sb(f"r1_{n}", [P, 1]) for n in ("m1", "x1", "m2", "x2", "sum", "inv")}
        y_f = sb("y_f", [P, D])
        out_sb = sb("out_sb", [P, D])

        bank = [stack.enter_context(nc.psum_tensor(f"bank{i}", [P, BANK], F32)) for i in range(8)]
        score_ps, flip_ps, value_ps, job_ps = bank[0:2], bank[2:4], bank[4:6], bank[6:8]
        up_ps = (score_ps, flip_ps)

        in_const, in_x = sem("in_const"), sem("in_x")
        in_attn = [sem(f"in_attn{n}") for n in range(2)]
        in_cross = [sem(f"in_cross{n}") for n in range(2)]
        in_null, in_ffn, in_ctx = sem("in_null"), sem("in_ffn"), sem("in_ctx")
        held = sem("held")
        ready_ones, ready_kb = sem("ready_ones"), sem("ready_kb")
        out_done = sem("out_done")

        def signals(prefix, names):
            return {name: sem(f"{prefix}_{name}") for name in names.split()}

        PER_LAYER = """scores maxed probs flipped flip_out_v flip_out_s values divided rsum job cur_a cur_x
            xt_a xt_x q_a k_a v_a q_x k_x v_x k_cur mixt_a mixt_x biased y_a y_x st_a st_x mv_a mv_x normed_x gp_a gp_x"""
        OWN_VALUES = " st_s mv_s st_z mv_z ya2 gp_z y_sum summed weigh mixed"
        sig = [signals(f"layer{n}", PER_LAYER + OWN_VALUES * n) for n in range(2)]

        moe = signals("moe", """ready turned0 turned1 x2t logits centred exp onehot cum put cleared scattered
            slots_in0 slots_in1 flipped slot_t up relu_s relu_v down out_t turned_back slot_out stored context own chain
            mv rstd gp done""")
        w_in = [sem(f"w_in{j}") for j in range(ROUND)]
        gathered = [sem(f"gathered{i}") for i in range(len(NORM_GROUPS))]
        f = signals("ffn", """cur turned xt gate gate_sb up0 up1 tanh tanh_s exp hid hid_s route routed flip_s
            flip0 flip1 ht_s ht0 ht1 down y st mv normed chain w gp out""")

        def hold(eng, semaphore, value):
            eng.wait_ge(semaphore, value)
            eng.sem_inc(held, 1)

        def mm(out_ap, lhs, rhs, first=True, last=True):
            return nc.tensor.matmul(out_ap, lhs, rhs, start=first, stop=last)

        def static(v):
            return isinstance(v, int)

        def batch_of(t, k):
            return t[:, k, :, :] if static(k) else t[:, bass.ds(k, 1), :, :].rearrange("p b n t -> p (b n) t")

        def mixes(layer, u):
            return u.kind == "x" or not LAYERS[layer]["own_values"]

        def pe_unit_scores(pe, layer, s, u):
            cfg = LAYERS[layer]
            n = cfg["blocks"] // 4 if u.kind == "a" else 2
            if u.group == 0 or u.group == 2 and n == 2:
                done = u.batch * n + (u.group // 2 + 1)
                pe.wait_ge(s["q_a"] if u.kind == "a" else s["q_x"], done)
                if u.kind == "a":
                    pe.wait_ge(s["k_a"], done)
                else:
                    pe.wait_ge(s["k_cur"], (u.batch + 1) * 16)
            if not static(u.b) or u.c >= 2:
                pe.wait_ge(s["probs"], u.count(2))
            for i, h in enumerate(heads_of(layer, u)):
                if u.kind == "a":
                    per = P // cfg["step"]
                    r, blk, n = cfg["step"] * (h % per), h // per, cfg["rows"]
                    q, k, keys = q_a[r:r + n, blk, :], k_a[r:r + n, blk, :], TOKENS
                else:
                    r, blk, keys = XD * (h % 2), h // 2, cfg["keys"]
                    q, k = q_x[r:r + XD, blk, :], k_cur[r:r + XD, blk, 0:keys]
                last = mm(score_ps[u.par][:, i * P:i * P + keys], q, k)
            last.then_inc(s["scores"], 1)

        def pe_unit_flip(pe, layer, s, u):
            keys = TOKENS if u.kind == "a" else LAYERS[layer]["keys"]
            pe.wait_ge(s["probs"], u.count())
            if has_turned(layer, u):
                pe.wait_ge((s["flip_out_v"], s["flip_out_s"])[u.par], half_turns(layer, u) - 1)
            for i in range(GROUP):
                last = nc.tensor.transpose(flip_ps[u.par][0:keys, i * P:(i + 1) * P], probs[:, u.par, i, 0:keys], ident)
            last.then_inc(s["flipped"], 1)

        def pe_unit_values(pe, layer, s, u):
            keys, v, w = (TOKENS, v_a, VD + 1) if u.kind == "a" else (LAYERS[layer]["keys"], batch_of(v_x, u.batch), XD + 1)
            pe.wait_ge((s["flip_out_v"], s["flip_out_s"])[u.par], half_turns(layer, u))
            if u.group == 0:
                if u.kind == "a":
                    pe.wait_ge(s["v_a"], u.batch + 1)
                else:
                    pe.wait_ge(s["v_x"], len(VALUE_JOBS))
            if has_turned(layer, u):
                pe.wait_ge(s["divided"], turns(layer, u, 2))
            for i, h in enumerate(heads_of(layer, u)):
                last = mm(value_ps[u.par][:, i * w:(i + 1) * w], probs_t[0:keys, u.par, i, :], v[0:keys, h, :])
            last.then_inc(s["values"], 1)

        def read_out(layer, s, j):
            name, k = j.name, j.batch
            if name[0:2] in ("qa", "ka"):
                return (s["q_a"] if name[0] == "q" else s["k_a"]), k * (LAYERS[layer]["blocks"] // 4) + (int(name[2]) + 1)
            if name[0:2] in ("kc", "vc"):
                return (s["k_x"] if name[0] == "k" else s["v_x"]), int(name[2:]) + 1
            if name[0:2] in ("qx", "tx"):
                credit = MIX_CREDIT if layer and name[0] == "t" else 0
                return (s["q_x"] if name[0] == "q" else s["mixt_x"]), k * 2 + (int(name[2]) + 1 + credit)
            if name == "yx":
                return s["y_x"], (k + 1 if LAYERS[layer]["stable"] else k + 2)
            return {"xa": s["xt_a"], "xx": s["xt_x"], "va": s["v_a"], "ta": s["mixt_a"], "ya": s["y_a"]}[name], k + 1

        def pe_context(layer, ps, name):
            i, part = divmod(int(name[2:]), 2)
            if name[0] == "k":
                return mm(ps[:, 0:HALF_CTX], wx(layer, "wk")[:, i * P:(i + 1) * P], ctx_all[:, part * HALF_CTX:(part + 1) * HALF_CTX])
            return mm(ps[0:CTX, :], ctx_all[:, i * CTX:(i + 1) * CTX], wx(layer, "wv")[:, part * BANK:(part + 1) * BANK])

        def context_out(copy, scale, ps, name):
            i, part = divmod(int(name[2:]), 2)
            if name[0] == "k":
                return scale(k_x[:, 4 * part:4 * part + 4, i, 0:CTX], ps[:, 0:HALF_CTX].rearrange("p (b t) -> p b t", b=4), X_SCALE)
            return copy(v_x[0:CTX, i, 8 * part:8 * part + 8, 0:XD], ps[0:CTX, :].rearrange("p (h d) -> p h d", h=8))

        def pe_job(pe, layer, s, j):
            cfg, ps, name, k = LAYERS[layer], job_ps[j.par], j.name, j.batch
            if name in NOT_JOBS:
                return
            if j.before:
                pe.wait_ge(*read_out(layer, s, j.before))
            if name == "kc0":
                pe.wait_ge(in_cross[layer], 16)
                pe.wait_ge(in_ctx, 16)
            if name == "xa":
                pe.wait_ge(s["cur_a"], k + 1)
                last = nc.tensor.transpose(ps[:, 0:P], cur_a[:], ident)
            elif name == "xx":
                pe.wait_ge(s["cur_x"], k + 1)
                last = nc.tensor.transpose(ps[:, 0:P], cur_x[:], ident)
            elif name[0:2] in ("qa", "ka"):
                if static(k) and k == 0:
                    pe.wait_ge(in_attn[layer], 16)
                pe.wait_ge(s["xt_a"], k + 1)
                n = int(name[2])
                w = wa(layer, "w" + name[0])
                for i in range(4):
                    last = mm(ps[:, i * P:(i + 1) * P], w[:, (4 * n + i) * P:(4 * n + i + 1) * P], xt_a[:])
            elif name == "va":
                last = mm(ps[:, 0:D], xt_a[:], wa(layer, "wv"))
            elif name[0:2] == "qx":
                if static(k) and k == 0:
                    pe.wait_ge(in_cross[layer], 16)
                pe.wait_ge(s["xt_x"], k + 1)
                n = int(name[2])
                w = wx(layer, "wq")
                for i in range(4):
                    last = mm(ps[:, i * P:(i + 1) * P], w[:, (4 * n + i) * P:(4 * n + i + 1) * P], xt_x[:])
            elif name[0:2] in ("kc", "vc"):
                last = pe_context(layer, ps, name)
            elif name == "ta":
                if cfg["own_values"]:
                    pe.wait_ge(s["mixed"], k + 1)
                else:
                    pe.wait_ge(s["divided"], 8 * k + 4 if static(k) and k == 0 else 8 * k)
                last = nc.tensor.transpose(ps[:, 0:P], mix_a[:, :, :].rearrange("p h d -> p (h d)"), ident)
            elif name[0:2] == "tx":
                n = int(name[2])
                if cfg["own_values"]:
                    pe.wait_ge(s["divided"], k * GROUPS + (2 * n + 2 + CREDIT))
                else:
                    pe.wait_ge(s["divided"], 8 * k + (10 + 2 * n if not static(k) or k < 7 else 6 + 2 * n))
                flat = mix_x[:, :, :].rearrange("p h d -> p (h d)")
                for i in range(4):
                    last = nc.tensor.transpose(ps[:, i * P:(i + 1) * P], flat[:, (4 * n + i) * P:(4 * n + i + 1) * P], ident)
            elif name == "ya":
                pe.wait_ge(s["mixt_a"], k + 1)
                last = mm(ps[:, 0:D], mixt_a[:], wa(layer, "wo"))
            elif name == "yx":
                w = wx(layer, "wo")
                for i in range(8):
                    if i % 4 == 0 and not layer:
                        pe.wait_ge(s["mixt_x"], k * 2 + (i // 4 + 1))
                    elif i == 0:
                        pe.wait_ge(s["mixt_x"], k * 2 + MIX_CREDIT)
                    last = mm(ps[:, 0:D], mixt_x[:, i, :], w[:, i * P:(i + 1) * P], i == 0, i == 7)
            last.then_inc(s["job"], 1)

        def pe_slot(pe, layer, s, scored, flipped, valued, jobs):
            if scored:
                pe_unit_scores(pe, layer, s, scored)
            if flipped and mixes(layer, flipped):
                pe_unit_flip(pe, layer, s, flipped)
            if valued and mixes(layer, valued):
                pe_unit_values(pe, layer, s, valued)
            for j in jobs:
                pe_job(pe, layer, s, j)

        def pe_layer(pe, layer):
            s = sig[layer]
            pe.wait_ge(in_const, 16)
            if layer:
                pe.wait_ge(in_null, 16)
                pe.wait_ge(s["k_x"], len(KEY_JOBS))
            if LAYERS[layer]["own_values"]:
                for semaphore in (s["flipped"], s["values"]):
                    pe.sem_inc(semaphore, CREDIT)
            for slot in slots_before(layer):
                pe_slot(pe, layer, s, *slot)
            with pe.Fori(0, LOOPS) as b:
                for slot in slots_loop(layer, b):
                    pe_slot(pe, layer, s, *slot)
            for slot in slots_after(layer):
                pe_slot(pe, layer, s, *slot)

        TURNS = ((0, range(0, 4)), (1, range(4, 8)), (2, range(8, 10)))
        turn_ps = (*flip_ps, value_ps[0])

        def pe_experts(pe):
            s = sig[0]
            pe.wait_ge(s["mixt_x"], 2 * BATCHES)
            pe.wait_ge(s["y_x"], BATCHES + 1)

            def values(first, last):
                for i in range(first, last):
                    if i >= 2:
                        pe.wait_ge(sig[1]["v_x"], i - 1)
                    pe_context(1, job_ps[i % 2], VALUE_JOBS[i]).then_inc(moe["context"], 1)

            pe.wait_ge(s["normed_x"], BATCHES - 1)
            for i in range(BATCHES):
                if i == BATCHES - 1:
                    pe.wait_ge(in_cross[1], 16)
                    values(0, EARLY_VALUES)
                    pe.wait_ge(s["normed_x"], BATCHES)
                last = nc.tensor.transpose(flip_ps[i // 4][:, (i % 4) * P:(i % 4 + 1) * P], xres[:, i, :], ident)
                if i % 4 == 3:
                    last.then_inc(moe["turned0"] if i == 3 else moe["turned1"], 1)
            for i in range(BATCHES):
                if i % 4 == 0:
                    pe.wait_ge(moe["x2t"], i // 4 + 1)
                last = mm(value_ps[0][:, i * EXPERTS:(i + 1) * EXPERTS], x2t[:, i, :], cut(const_sb, C_COLS, "wr"))
            last.then_inc(moe["logits"], 1)
            pe.wait_ge(moe["ready"], 1)
            pe.wait_ge(moe["onehot"], 1)
            cum = value_ps[1][:, 0:BATCHES * EXPERTS].rearrange("p (b e) -> p b e", b=BATCHES)
            mm(cum, tri_b[:], onehot_b[:, :, :], True, False)
            for i in range(BATCHES - 1):
                n = BATCHES - 1 - i
                last = mm(cum[:, i + 1:BATCHES, :], ones_b[:], onehot_b[:, i:i + 1, :].to_broadcast([P, n, EXPERTS]),
                          False, i == BATCHES - 2)
            last.then_inc(moe["cum"], 1)

            values(EARLY_VALUES, len(VALUE_JOBS))
            for i, (bank_, tiles) in enumerate(TURNS):
                pe.wait_ge(moe["slots_in1"] if i else moe["slots_in0"], 16)
                for n, t in enumerate(tiles):
                    last = nc.tensor.transpose(turn_ps[bank_][:, n * P:(n + 1) * P], slot_in[:, t, :], ident)
                last.then_inc(moe["flipped"], 1)

            def up(e, j):
                if static(e) or j == 0:
                    pe.wait_ge(moe["slot_t"], len(TURNS))
                pe.wait_ge(w_in[j], e * 8 + (32 - 8 * j))
                if not static(e) or e > 0:
                    pe.wait_ge(moe["relu_s"], e)
                    pe.wait_ge(moe["relu_v"], e)
                for fb in range(FB):
                    last = mm(score_ps[fb // 2][:, (fb % 2) * CAP:(fb % 2 + 1) * CAP], w1_sb[:, j, fb * P:(fb + 1) * P],
                              slot_t[:, bass.ds(e * CAP, CAP)])
                    if fb % 2:
                        last.then_inc(moe["up"], 1)

            def down(e, j):
                pe.wait_ge(moe["relu_s"], e + 1)
                pe.wait_ge(moe["relu_v"], e + 1)
                if not static(e) or e > 1:
                    pe.wait_ge(moe["out_t"], e - 1)
                for fb in range(FB):
                    last = mm(value_ps[j % 2][:, 0:CAP], w2_sb[:, j, fb, :], hidden[:, j % 2, fb, :], fb == 0, fb == FB - 1)
                last.then_inc(moe["down"], 1)

            def back_turn(i):
                pe.wait_ge(moe["out_t"], i * ROUND + ROUND)
                for t in range(ROUND_TILES):
                    last = nc.tensor.transpose(job_ps[t // 4][:, (t % 4) * P:(t % 4 + 1) * P], out_t[:, t * P:(t + 1) * P], ident)
                last.then_inc(moe["turned_back"], 1)

            def one_round(i):
                e = i * ROUND
                up(e, 0)
                for j in range(1, ROUND):
                    up(e + j, j)
                    down(e + (j - 1), j - 1)
                down(e + (ROUND - 1), ROUND - 1)
                back_turn(i)

            for i in range(ROUNDS):
                one_round(i)
            pe.wait_ge(moe["slot_out"], 2 * ROUNDS)
            for i, name in enumerate(KEY_JOBS):
                if i >= 2:
                    pe.wait_ge(sig[1]["k_x"], i - 1)
                pe_context(1, job_ps[i % 2], name).then_inc(moe["context"], 1)

        def pe_ffn(pe):
            pe.wait_ge(in_ffn, 16)
            gate_w, ws = cut(ffn_sb, F_COLS, "gate"), cut(ffn_sb, F_COLS, "ws")
            wg, wu, wd = (cut(ffn_sb, F_COLS, n) for n in ("wg", "wu", "wd"))

            def turn(k):
                pe.wait_ge(f["cur"], k + 1)
                if not static(k) or k > 0:
                    pe.wait_ge(f["gate_sb"], k)
                nc.tensor.transpose(job_ps[0][:, 0:P], cur_a[:], ident).then_inc(f["turned"], 1)

            def up(k):
                pe.wait_ge(f["xt"], k + 1)
                mm(job_ps[0][:, 0:E2], xt_f[:], gate_w)
                mm(job_ps[0][:, E2:E2 + 2 * M2], xt_f[:], ws).then_inc(f["gate"], 1)
                for c in range(2):
                    if not static(k) or k > 0:
                        pe.wait_ge(f["hid"], k * 2 - 1 + c)
                    mm(up_ps[c][0][:, :], xt_f[:], wg[:, c * BANK:(c + 1) * BANK])
                    mm(up_ps[c][1][:, :], xt_f[:], wu[:, c * BANK:(c + 1) * BANK]).then_inc(f["up0"] if c == 0 else f["up1"], 1)

            def down(k):
                if not static(k) or k > 0:
                    pe.wait_ge(f["y"], k)
                hold(pe, f["hid_s"], k + 1)
                nc.tensor.transpose(job_ps[1][0:M2, D:D + P], hid_s2[:], ident).then_inc(f["flip_s"], 1)
                for c in range(2):
                    pe.wait_ge(f["routed"], k * 2 + (1 + c))
                    for i in range(4):
                        last = nc.tensor.transpose(value_ps[c][:, i * P:(i + 1) * P], hid_r[:, c, i * P:(i + 1) * P], ident)
                    last.then_inc(f["flip0"] if c == 0 else f["flip1"], 1)
                pe.wait_ge(f["ht_s"], k + 1)
                mm(job_ps[1][:, 0:D], ht_s[:], wd[0:M2, 8 * D:9 * D], True, False)
                for i in range(8):
                    if i % 4 == 0:
                        pe.wait_ge(f["ht1"] if i else f["ht0"], k + 1)
                    last = mm(job_ps[1][:, 0:D], ht[:, i, :], wd[:, i * D:(i + 1) * D], False, i == 7)
                last.then_inc(f["down"], 1)

            pe.wait_ge(sig[1]["mixt_x"], 2 * BATCHES + MIX_CREDIT)
            pe.wait_ge(sig[1]["y_x"], BATCHES + 1)
            turn(0)
            up(0)
            turn(1)
            with pe.Fori(1, BATCHES - 1) as k:
                up(k)
                turn(k + 1)
                down(k - 1)
            up(BATCHES - 1)
            down(BATCHES - 2)
            down(BATCHES - 1)

        def act_unit_exp(act, layer, s, u):
            keys = TOKENS if u.kind == "a" else LAYERS[layer]["keys"]
            to = probs if mixes(layer, u) else probs_a
            act.wait_ge(s["maxed"], u.count())
            if not mixes(layer, u):
                act.wait_ge(s["summed"], turns(layer, u, 2))
            elif has_turned(layer, u):
                act.wait_ge(s["flipped"], turns(layer, u, 2))
            for i in range(GROUP):
                last = nc.scalar.activation(to[:, u.par, i, 0:keys], score_ps[u.par][:, i * P:i * P + keys], ACT.Exp,
                                            bias=negmax[:, u.par, i:i + 1])
            last.then_inc(s["probs"], 1)

        def act_unit_flip_out(act, layer, s, u):
            keys = TOKENS if u.kind == "a" else LAYERS[layer]["keys"]
            act.wait_ge(s["flipped"], turns(layer, u))
            if has_turned(layer, u):
                act.wait_ge(s["values"], turns(layer, u, 2))
            nc.scalar.copy(probs_t[0:keys, u.par, :, :],
                           flip_ps[u.par][0:keys, :].rearrange("p (h t) -> p h t", h=GROUP)).then_inc(s["flip_out_s"], 1)

        def act_job(act, layer, s, j):
            cfg, ps, name, k = LAYERS[layer], job_ps[j.par], j.name, j.batch
            if name not in ("xa", "xx", "ta", "tx0", "tx1", "ka0", "ka1") and name[0:2] != "kc":
                return
            act.wait_ge(s["job"], j.count())
            blocks = ps[:, :].rearrange("p (n t) -> p n t", n=4)
            if name == "xa":
                done = nc.scalar.copy(xt_a[:], ps[:, 0:P]), s["xt_a"]
            elif name == "xx" and cfg["stable"]:
                done = nc.scalar.activation(xt_x[:], ps[:, 0:P], ACT.Copy, scale=wx(layer, "col")), s["xt_x"]
            elif name == "xx":
                done = nc.scalar.copy(xt_x[:], ps[:, 0:P]), s["xt_x"]
            elif name == "ta":
                done = nc.scalar.copy(mixt_a[:], ps[:, 0:P]), s["mixt_a"]
            elif name[0:2] == "tx":
                n = int(name[2])
                done = nc.scalar.copy(mixt_x[:, 4 * n:4 * n + 4, :], blocks), s["mixt_x"]
            elif name[0:2] == "ka":
                n = int(name[2])
                if static(k) and k == 0:
                    act.wait_ge(ready_kb, layer + 1)
                for i in range(4):
                    last = nc.scalar.activation(k_a[:, 4 * n + i, :], blocks[:, i, :], ACT.Identity, scale=cfg["scale"],
                                                bias=kb_scaled[:, 4 * n + i:4 * n + i + 1])
                done = last, s["k_a"]
            else:
                done = context_out(nc.scalar.copy, nc.scalar.mul, ps, name), s["k_x"]
            done[0].then_inc(done[1], 1)

        def act_slot(act, layer, s, scored, flipped, valued, jobs):
            if flipped and flipped.par == 1 and mixes(layer, flipped):
                act_unit_flip_out(act, layer, s, flipped)
            early = [j for j in jobs if j.name in ("xx", "tx0") and layer]
            for j in early:
                act_job(act, layer, s, j)
            if scored:
                act_unit_exp(act, layer, s, scored)
            for j in jobs:
                if j not in early:
                    act_job(act, layer, s, j)

        def act_layer(act, layer):
            s = sig[layer]
            if LAYERS[layer]["own_values"]:
                act.sem_inc(s["flip_out_s"], CREDIT // 2)
                act.sem_inc(s["mixt_x"], MIX_CREDIT)
            for slot in slots_before(layer):
                act_slot(act, layer, s, *slot)
            with act.Fori(0, LOOPS) as b:
                for slot in slots_loop(layer, b):
                    act_slot(act, layer, s, *slot)
            for slot in slots_after(layer):
                act_slot(act, layer, s, *slot)

        def act_experts(act):
            def values(first, last):
                for i in range(first, last):
                    act.wait_ge(moe["context"], i + 1)
                    context_out(nc.scalar.copy, nc.scalar.mul, job_ps[i % 2], VALUE_JOBS[i]).then_inc(sig[1]["v_x"], 1)

            for i in range(2):
                if i == 1:
                    values(0, EARLY_VALUES)
                act.wait_ge(moe["turned1"] if i else moe["turned0"], 1)
                nc.scalar.copy(x2t[:, 4 * i:4 * i + 4, :], flip_ps[i][:, :].rearrange("p (b t) -> p b t", b=4)).then_inc(moe["x2t"], 1)
            act.wait_ge(moe["centred"], 1)
            nc.scalar.activation(lg["exp"][:], lg["centred"][:], ACT.Exp).then_inc(moe["exp"], 1)

            values(EARLY_VALUES, len(VALUE_JOBS))
            for i, (bank_, tiles) in enumerate(TURNS):
                act.wait_ge(moe["flipped"], i + 1)
                nc.scalar.copy(slot_t[:, tiles[0] * P:(tiles[-1] + 1) * P], turn_ps[bank_][:, 0:len(tiles) * P])\
                    .then_inc(moe["slot_t"], 1)

            def relu(e, j):
                act.wait_ge(moe["up"], e * 2 + 1)
                if not static(e) or e > 1:
                    act.wait_ge(moe["down"], e - 1)
                nc.scalar.activation(hidden[:, j % 2, 0:2, :], score_ps[0][:, 0:2 * CAP].rearrange("p (n t) -> p n t", n=2), ACT.Relu)\
                    .then_inc(moe["relu_s"], 1)

            def one_round(i):
                for j in range(ROUND):
                    relu(i * ROUND + j, j)
                act.wait_ge(moe["turned_back"], i + 1)
                if not static(i) or i > 0:
                    act.wait_ge(moe["stored"], i * 16)
                nc.scalar.copy(slot_out[:, 0:4, :], job_ps[0][:, :].rearrange("p (t d) -> p t d", t=4)).then_inc(moe["slot_out"], 1)

            for i in range(ROUNDS):
                one_round(i)
            for i, name in enumerate(KEY_JOBS):
                act.wait_ge(moe["context"], len(VALUE_JOBS) + i + 1)
                context_out(nc.scalar.copy, nc.scalar.mul, job_ps[i % 2], name).then_inc(sig[1]["k_x"], 1)

        def act_ffn(act):
            def turn(k):
                act.wait_ge(f["turned"], k + 1)
                nc.scalar.copy(xt_f[:], job_ps[0][:, 0:P]).then_inc(f["xt"], 1)

            def squash(k):
                act.wait_ge(f["gate_sb"], k + 1)
                nc.scalar.activation(r16["exp"][:], gate_sb[:, 0:E2], ACT.Exp, scale=-1.0).then_inc(f["exp"], 1)
                nc.scalar.activation(tanh_s[:], gate_sb[:, E2:E2 + M2], ACT.Tanh, scale=0.5).then_inc(f["tanh_s"], 1)
                for c in range(2):
                    act.wait_ge(f["up1"] if c else f["up0"], k + 1)
                    nc.scalar.activation(tanh_g[:, c, :], up_ps[c][0][:, :], ACT.Tanh, scale=0.5).then_inc(f["tanh"], 1)

            def flip(k):
                act.wait_ge(f["flip_s"], k + 1)
                nc.scalar.copy(ht_s[:], job_ps[1][0:M2, D:D + P]).then_inc(f["ht_s"], 1)
                for c in range(2):
                    act.wait_ge(f["flip1"] if c else f["flip0"], k + 1)
                    nc.scalar.copy(ht[:, 4 * c:4 * c + 4, :], value_ps[c][:, :].rearrange("p (n t) -> p n t", n=4))\
                        .then_inc(f["ht1"] if c else f["ht0"], 1)

            turn(0)
            squash(0)
            turn(1)
            with act.Fori(1, BATCHES - 1) as k:
                squash(k)
                turn(k + 1)
                flip(k - 1)
            squash(BATCHES - 1)
            flip(BATCHES - 2)
            flip(BATCHES - 1)

        def dve_unit_max(dve, layer, s, u):
            keys = TOKENS if u.kind == "a" else LAYERS[layer]["keys"]
            dve.wait_ge(s["scores"], u.count())
            nc.vector.tensor_reduce(negmax[:, u.par, :],
                                    score_ps[u.par][:, :].rearrange("p (h k) -> p h k", h=GROUP)[:, :, 0:keys],
                                    axis=AX_X, op=ALU.max, negate=True).then_inc(s["maxed"], 1)

        def dve_unit_flip_out(dve, layer, s, u):
            keys = TOKENS if u.kind == "a" else LAYERS[layer]["keys"]
            dve.wait_ge(s["flipped"], turns(layer, u))
            if has_turned(layer, u):
                dve.wait_ge(s["values"], turns(layer, u, 2))
            nc.vector.tensor_copy(probs_t[0:keys, u.par, :, :],
                                  flip_ps[u.par][0:keys, :].rearrange("p (h t) -> p h t", h=GROUP)).then_inc(s["flip_out_v"], 1)

        def dve_unit_sum(dve, layer, s, u):
            hs = heads_of(layer, u)
            dve.wait_ge(s["probs"], u.count())
            nc.vector.tensor_reduce(sums_a[:, hs.start:hs[-1] + 1:hs.step], probs_a[:, u.par, :, :], axis=AX_X, op=ALU.add)\
                .then_inc(s["summed"], 1)

        def dve_own_values(dve, s, u):
            k = u.batch
            dve.wait_ge(s["summed"], k * GROUPS + (GROUPS + CREDIT))
            nc.vector.reciprocal(inv_a[:], sums_a[:]).then_inc(s["weigh"], 1)
            dve.wait_ge(s["weigh"], k * 2 + 1)
            nc.vector.tensor_tensor(weight_a[:], sums_a[:], inv_a[:], ALU.mult).then_inc(s["weigh"], 1)
            if not static(k) or k > 0:
                dve.wait_ge(s["mixt_a"], k)
            dve.wait_ge(s["v_a"], k + 1)
            dve.wait_ge(s["weigh"], k * 2 + 2)
            nc.vector.tensor_tensor(mix_a[:, :, :], v_a[:, :, 0:VD], weight_a[:].unsqueeze(2).to_broadcast([P, HEADS, VD]), ALU.mult)\
                .then_inc(s["mixed"], 1)

        def dve_unit_rsum(dve, layer, s, u):
            w = (VD if u.kind == "a" else XD) + 1
            dve.wait_ge(s["values"], turns(layer, u))
            nc.vector.reciprocal(rsum[:, u.par, :].unsqueeze(2),
                                 value_ps[u.par][:, 0:GROUP * w].rearrange("p (h d) -> p h d", h=GROUP)[:, :, w - 1:w])\
                .then_inc(s["rsum"], 1)

        def dve_unit_divide(dve, layer, s, u):
            w, mix = (VD, mix_a) if u.kind == "a" else (XD, mix_x)
            if u.kind == "a" and u.group == 0 and static(u.batch) and u.batch == 1:
                dve.wait_ge(s["mixt_a"], 1)
            dve.wait_ge(s["rsum"], turns(layer, u))
            hs = heads_of(layer, u)
            nc.vector.tensor_tensor(mix[:, hs.start:hs[-1] + 1:hs.step, :],
                                    value_ps[u.par][:, 0:GROUP * (w + 1)].rearrange("p (h d) -> p h d", h=GROUP)[:, :, 0:w],
                                    rsum[:, u.par, :].unsqueeze(2).to_broadcast([P, GROUP, w]), ALU.mult)\
                .then_inc(s["divided"], 1)

        def dve_stats(dve, stats_done, kind, src, k):
            nc.vector.bn_stats(bns[kind][:], src).then_inc(stats_done, 1)
            hold(dve, stats_done, k + 1)
            return nc.vector.bn_aggr(mv[kind][:], bns[kind][:])

        def dve_stable(dve, stats_done, kind, src, k):
            nc.vector.tensor_reduce(rmax[kind][:], src, axis=AX_X, op=ALU.max)
            nc.vector.bn_stats(bns[kind][:], src).then_inc(stats_done, 1)
            hold(dve, stats_done, k + 1)
            nc.vector.reciprocal(rinv[kind][:], rmax[kind][:])
            return nc.vector.bn_aggr(mv[kind][:], bns[kind][:])

        def dve_job(dve, layer, s, j):
            cfg, ps, name, k = LAYERS[layer], job_ps[j.par], j.name, j.batch
            if name == "sa" and cfg["stable"]:
                dve.wait_ge(s["ya2"], k + 1)
                dve_stable(dve, s["st_s"], "s", normed[:], k).then_inc(s["mv_s"], 1)
            if name == "sz":
                dve.wait_ge(s["y_x"], k + 1)
                dve_stable(dve, s["st_z"], "z", y["x"][:], k).then_inc(s["mv_z"], 1)
            if name == "sx":
                dve.wait_ge(s["y_sum"], k + 1)
                dve_stats(dve, s["st_x"], "x", y["x"][:], k).then_inc(s["mv_x"], 1)
            if name[0:2] not in ("qa", "va", "qx", "vc", "ya", "yx"):
                return
            dve.wait_ge(s["job"], j.count())
            blocks = ps[:, :].rearrange("p (n t) -> p n t", n=4)
            if name[0:2] == "qa":
                n = int(name[2])
                nc.vector.tensor_tensor(q_a[:, 4 * n:4 * n + 4, :], blocks,
                                        wa(layer, "bq")[:, 4 * n:4 * n + 4].unsqueeze(2).to_broadcast([P, 4, TOKENS]), ALU.add)\
                    .then_inc(s["q_a"], 1)
            elif name == "va":
                if cfg["own_values"] and (not static(k) or k > 0):
                    dve.wait_ge(s["mixed"], k)
                nc.vector.tensor_tensor(v_a[:, :, 0:VD], ps[:, 0:D].rearrange("p (h d) -> p h d", h=HEADS),
                                        wa(layer, "bv").rearrange("p (h d) -> p h d", h=HEADS), ALU.add)\
                    .then_inc(s["v_a"], 1)
            elif name[0:2] == "qx":
                n = int(name[2])
                nc.vector.tensor_copy(q_x[:, 4 * n:4 * n + 4, :], blocks)\
                    .then_inc(s["q_x"], 1)
            elif name[0:2] == "vc":
                context_out(nc.vector.tensor_copy, None, ps, name).then_inc(s["v_x"], 1)
            elif name == "ya":
                dve.wait_ge(s["biased"], k + 1)
                nc.vector.tensor_tensor(y["a"][:], ps[:, 0:D], xres[:, bass.ds(k, 1), :].rearrange("p b d -> p (b d)"), ALU.add)\
                    .then_inc(s["y_a"], 1)
                dve.wait_ge(s["y_a"], k + 1)
                dve_stats(dve, s["st_a"], "a", y["a"][:], k).then_inc(s["mv_a"], 1)
            elif cfg["stable"]:
                if static(k) and k == BATCHES:
                    dve.wait_ge(s["normed_x"], k - 1)
                nc.vector.tensor_copy(y["x"][:], ps[:, 0:D]).then_inc(s["y_x"], 1)
            else:
                if static(k) and k == BATCHES - 1:
                    dve.wait_ge(s["normed_x"], k)
                nc.vector.tensor_tensor(y["x"][:], ps[:, 0:D], xres[:, bass.ds(k, 1), :].rearrange("p b d -> p (b d)"), ALU.add)\
                    .then_inc(s["y_x"], 1)
                dve.wait_ge(s["y_x"], k + 2)
                dve_stats(dve, s["st_x"], "x", y["x"][:], k).then_inc(s["mv_x"], 1)

        def dve_slot(dve, layer, s, scored, flipped, valued, jobs):
            if scored:
                dve_unit_max(dve, layer, s, scored)
            if flipped and not mixes(layer, flipped):
                dve_unit_sum(dve, layer, s, flipped)
            elif flipped and flipped.par == 0:
                dve_unit_flip_out(dve, layer, s, flipped)
            if valued and mixes(layer, valued):
                dve_unit_rsum(dve, layer, s, valued)
                dve_unit_divide(dve, layer, s, valued)
            early = [j for j in jobs if j.name in EARLY_JOBS]
            for j in early:
                dve_job(dve, layer, s, j)
            if flipped and flipped.group == GROUPS - 1 and not mixes(layer, flipped):
                dve_own_values(dve, s, flipped)
            for j in jobs:
                if j not in early:
                    dve_job(dve, layer, s, j)

        def dve_layer(dve, layer):
            s = sig[layer]
            dve.wait_ge(in_attn[layer], 16)
            nb = LAYERS[layer]["blocks"]
            if LAYERS[layer]["stable"]:
                dve.wait_ge(in_cross[layer], 16)
                dve.sem_inc(s["flip_out_v"], CREDIT // 2)
                for semaphore in (s["rsum"], s["divided"], s["summed"]):
                    dve.sem_inc(semaphore, CREDIT)
                nc.vector.tensor_scalar(k_x[:, :, :, CTX], wx(layer, "null").unsqueeze(1).to_broadcast([P, BATCHES, 8]), X_SCALE,
                                        None, ALU.mult)
            nc.vector.tensor_scalar(kb_scaled[:, 0:nb], wa(layer, "bk"), LAYERS[layer]["scale"], None, ALU.mult)\
                .then_inc(ready_kb, 1)
            dve.sem_inc(s["y_sum"] if LAYERS[layer]["stable"] else s["y_x"], 1)
            for slot in slots_before(layer):
                dve_slot(dve, layer, s, *slot)
            with dve.Fori(0, LOOPS) as b:
                for slot in slots_loop(layer, b):
                    dve_slot(dve, layer, s, *slot)
            for slot in slots_after(layer):
                dve_slot(dve, layer, s, *slot)

        def dve_experts(dve):
            count = [0]

            def step(ins):
                count[0] += 1
                ins.then_inc(moe["chain"], 1)
                dve.wait_ge(moe["chain"], count[0])

            def wide(t):
                return t[:].unsqueeze(2).to_broadcast([P, BATCHES, EXPERTS])

            logits = value_ps[0][:, 0:BATCHES * EXPERTS].rearrange("p (b e) -> p b e", b=BATCHES)
            rev = cut(const_sb, C_COLS, "rev8").rearrange("p (b e) -> p b e", b=BATCHES)
            nc.vector.tensor_copy(tri_b[:], cut(const_sb, C_COLS, "tri"))
            dve.wait_ge(moe["logits"], 1)
            step(nc.vector.tensor_reduce(tok["max"][:], logits, axis=AX_X, op=ALU.max))
            nc.vector.tensor_tensor(lg["centred"][:], logits, wide(tok["max"]), ALU.subtract).then_inc(moe["centred"], 1)
            dve.wait_ge(moe["centred"], 1)
            step(nc.vector.scalar_tensor_tensor(lg["pick"][:], lg["centred"][:], 0.0, rev, ALU.is_ge, ALU.mult))
            step(nc.vector.tensor_reduce(tok["pick"][:], lg["pick"][:], axis=AX_X, op=ALU.max))
            step(nc.vector.tensor_tensor(lg["onehot"][:], lg["pick"][:], wide(tok["pick"]), ALU.is_equal))
            nc.vector.tensor_copy(onehot_b[:], lg["onehot"][:]).then_inc(moe["onehot"], 1)
            dve.wait_ge(moe["exp"], 1)
            step(nc.vector.tensor_reduce(tok["sum"][:], lg["exp"][:], axis=AX_X, op=ALU.add))
            step(nc.vector.reciprocal(tok["prob"][:], tok["sum"][:]))
            step(nc.vector.tensor_scalar(tok["base"][:], tok["pick"][:], -float(CAP), float(CAP * EXPERTS - 1), ALU.mult, ALU.add))
            dve.wait_ge(moe["cum"], 1)
            cum = value_ps[1][:, 0:BATCHES * EXPERTS].rearrange("p (b e) -> p b e", b=BATCHES)
            step(nc.vector.tensor_tensor(lg["at"][:], cum, lg["onehot"][:], ALU.mult))
            step(nc.vector.tensor_reduce(tok["pos"][:], lg["at"][:], axis=AX_X, op=ALU.add))
            step(nc.vector.tensor_scalar(tok["kept"][:], tok["pos"][:], CAP + 0.5, None, ALU.is_le))
            step(nc.vector.scalar_tensor_tensor(tok["slot"][:], tok["pos"][:], float(CAP), tok["base"][:], ALU.min, ALU.add))
            step(nc.vector.tensor_scalar(tok["lost"][:], tok["kept"][:], -1.0, 1.0, ALU.mult, ALU.add))
            step(nc.vector.tensor_tensor(tok["spare"][:], cut(const_sb, C_COLS, "token"), tok["lost"][:], ALU.mult))
            step(nc.vector.tensor_tensor(tok["apart"][:], tok["slot"][:], tok["kept"][:], ALU.mult))
            step(nc.vector.tensor_tensor(tok["put"][:], tok["apart"][:], tok["spare"][:], ALU.add))
            nc.vector.tensor_copy(get_at[:], tok["slot"][:])
            nc.vector.tensor_copy(put_at[:], tok["put"][:]).then_inc(moe["put"], 1)
            step(nc.vector.tensor_tensor(tok["factor"][:], tok["kept"][:], tok["prob"][:], ALU.mult))
            step(nc.vector.tensor_scalar(tok["own"][:], tok["lost"][:], 1.0, None, ALU.add))
            for i in range(BATCHES):
                last = nc.vector.tensor_scalar(own[:, i, :], xres[:, i, :], tok["own"][:, i:i + 1], None, ALU.mult)
            last.then_inc(moe["own"], 1)

            def relu(e, j):
                dve.wait_ge(moe["up"], e * 2 + 2)
                if not static(e) or e > 1:
                    dve.wait_ge(moe["down"], e - 1)
                nc.vector.tensor_scalar(hidden[:, j % 2, 2:4, :], score_ps[1][:, 0:2 * CAP].rearrange("p (n t) -> p n t", n=2), 0.0,
                                        None, ALU.max).then_inc(moe["relu_v"], 1)

            def out_copy(e, j):
                dve.wait_ge(moe["down"], e + 1)
                if not static(e) or e >= ROUND:
                    if j == 0:
                        dve.wait_ge(moe["turned_back"], 1)
                nc.vector.tensor_copy(out_t[:, j * CAP:(j + 1) * CAP], value_ps[j % 2][:, 0:CAP]).then_inc(moe["out_t"], 1)

            def one_round(i):
                e = i * ROUND
                relu(e, 0)
                for j in range(1, ROUND):
                    relu(e + j, j)
                    out_copy(e + (j - 1), j - 1)
                out_copy(e + (ROUND - 1), ROUND - 1)
                dve.wait_ge(moe["turned_back"], i + 1)
                if not static(i) or i > 0:
                    dve.wait_ge(moe["stored"], i * 16)
                nc.vector.tensor_copy(slot_out[:, 4, :], job_ps[1][:, 0:P]).then_inc(moe["slot_out"], 1)

            for i in range(ROUNDS):
                one_round(i)
            dve.wait_ge(moe["own"], 1)
            def mark(ins):
                count[0] += 1
                ins.then_inc(moe["chain"], 1)

            def stats(n):
                group = NORM_GROUPS[n]
                dve.wait_ge(gathered[n], 16 * len(group))
                for i in group:
                    mark(nc.vector.scalar_tensor_tensor(y8[:, i, :], back[:, i, :], tok["factor"][:, i:i + 1], own[:, i, :], ALU.mult, ALU.add))
                dve.wait_ge(moe["chain"], count[0])
                for i in group:
                    mark(nc.vector.bn_stats(bns8[:, i, :], y8[:, i, :]))
                dve.wait_ge(moe["chain"], count[0])
                for i in group:
                    last = nc.vector.bn_aggr(mv8[:, i, :], bns8[:, i, :])
                last.then_inc(moe["mv"], 1)

            def normed8(n):
                dve.wait_ge(moe["rstd"], n + 1)
                for i in NORM_GROUPS[n]:
                    nc.vector.tensor_scalar(xres[:, i, :], y8[:, i, :], mv8[:, i, 0:1], rstd8[:, i:i + 1], ALU.subtract, ALU.mult)\
                        .then_inc(moe["done"], 1)

            stats(0)
            stats(1)
            normed8(0)
            stats(2)
            normed8(1)
            normed8(2)

        def tile_of(k):
            return xres[:, bass.ds(k, 1), :].rearrange("p b d -> p (b d)")

        def dve_ffn(dve):
            rev = cut(const_sb, C_COLS, "rev16")
            N_ROUTE = 13

            def gates(k):
                dve.wait_ge(f["gate"], k + 1)
                nc.vector.tensor_copy(gate_sb[:], job_ps[0][:, 0:E2 + 2 * M2]).then_inc(f["gate_sb"], 1)

            def front(k):
                done = [0]

                def mark(ins):
                    done[0] += 1
                    ins.then_inc(f["chain"], 1)

                def settled():
                    dve.wait_ge(f["chain"], k * N_ROUTE + done[0])

                def step(ins):
                    mark(ins)
                    settled()

                def first_best(best, place, from_, key):
                    step(nc.vector.tensor_reduce(r1[best][:], from_, axis=AX_X, op=ALU.max))
                    step(nc.vector.scalar_tensor_tensor(r16[key][:], from_, r1[best][:], rev, ALU.is_equal, ALU.mult))
                    step(nc.vector.tensor_reduce(r1[place][:], r16[key][:], axis=AX_X, op=ALU.max))

                def gated(c):
                    dve.wait_ge(f["tanh"], k * 2 + (1 + c))
                    nc.vector.scalar_tensor_tensor(tanh_g[:, c, :], tanh_g[:, c, :], 1.0, up_ps[c][0][:, :], ALU.add, ALU.mult)\
                        .then_inc(f["w"], 1)

                def times_up(c):
                    dve.wait_ge(f["w"], k * 4 + (2 + c))
                    if not static(k) or k > 0:
                        dve.wait_ge(f["routed"], k * 2 - (1 - c))
                    nc.vector.tensor_tensor(hid[:, c, :], tanh_g[:, c, :], up_ps[c][1][:, :], ALU.mult).then_inc(f["hid"], 1)

                gates(k)
                dve.wait_ge(f["exp"], k + 1)
                step(nc.vector.tensor_scalar(r16["sum"][:], r16["exp"][:], 1.0, None, ALU.add))
                mark(nc.vector.reciprocal(r16["score"][:], r16["sum"][:]))
                dve.wait_ge(f["tanh_s"], k + 1)
                nc.vector.scalar_tensor_tensor(hid_s[:], tanh_s[:], 1.0, gate_sb[:, E2:E2 + M2], ALU.add, ALU.mult).then_inc(f["w"], 1)
                settled()
                first_best("m1", "x1", r16["score"][:], "w1")
                mark(nc.vector.tensor_scalar(r16["one1"][:], r16["w1"][:], r1["x1"][:], None, ALU.is_equal))
                dve.wait_ge(f["w"], k * 4 + 1)
                if not static(k) or k > 0:
                    dve.wait_ge(f["flip_s"], k)
                nc.vector.scalar_tensor_tensor(hid_s2[:], hid_s[:], 0.5, gate_sb[:, E2 + M2:], ALU.mult, ALU.mult)\
                    .then_inc(f["hid_s"], 1)
                settled()
                mark(nc.vector.scalar_tensor_tensor(r16["rest"][:], r16["one1"][:], -4.0, r16["score"][:], ALU.mult, ALU.add))
                gated(0)
                settled()
                mark(nc.vector.tensor_reduce(r1["m2"][:], r16["rest"][:], axis=AX_X, op=ALU.max))
                times_up(0)
                settled()
                step(nc.vector.scalar_tensor_tensor(r16["w2"][:], r16["rest"][:], r1["m2"][:], rev, ALU.is_equal, ALU.mult))
                mark(nc.vector.tensor_reduce(r1["x2"][:], r16["w2"][:], axis=AX_X, op=ALU.max))
                gated(1)
                settled()
                mark(nc.vector.tensor_scalar(r16["two"][:], r16["w2"][:], r1["x2"][:], r1["m2"][:], ALU.is_equal, ALU.mult))
                times_up(1)
                settled()
                step(nc.vector.tensor_scalar(r1["sum"][:], r1["m1"][:], r1["m2"][:], 1e-20, ALU.add, ALU.add))
                step(nc.vector.reciprocal(r1["inv"][:], r1["sum"][:]))
                nc.vector.scalar_tensor_tensor(r16["sum"][:], r16["one1"][:], r1["m1"][:], r16["two"][:], ALU.mult, ALU.add)\
                    .then_inc(f["w"], 1)
                assert done[0] == N_ROUTE
                dve.wait_ge(f["w"], k * 4 + 4)
                if not static(k) or k > 0:
                    dve.wait_ge(f["routed"], k * 2)
                nc.vector.tensor_scalar(r16["route"][:], r16["sum"][:], r1["inv"][:], 0.5 * ROUTE_SCALE, ALU.mult, ALU.mult)\
                    .then_inc(f["route"], 1)

            def end(k):
                dve.wait_ge(f["down"], k + 1)
                if not static(k) or k > 0:
                    dve.wait_ge(f["normed"], k)
                nc.vector.tensor_tensor(y_f[:], job_ps[1][:, 0:D], tile_of(k), ALU.add).then_inc(f["y"], 1)
                dve.wait_ge(f["y"], k + 1)
                nc.vector.bn_stats(bns["x"][:], y_f[:]).then_inc(f["st"], 1)
                hold(dve, f["st"], k + 1)
                nc.vector.bn_aggr(mv["x"][:], bns["x"][:]).then_inc(f["mv"], 1)

            front(0)
            dve_job(dve, 1, sig[1], Job("sx", BATCHES))
            front(1)
            end(0)
            with dve.Fori(2, BATCHES) as k:
                front(k)
                end(k - 1)
            end(BATCHES - 1)

        def steps_of(gp, semaphore, k, n):
            done = [0]

            def step(ins):
                done[0] += 1
                assert done[0] <= n
                ins.then_inc(semaphore, 1)
                hold(gp, semaphore, k * n + done[0])
            return step

        def gp_scale(gp, step, var):
            step(gp.tensor_scalar(ve[:], var, LN_EPS, None, ALU.add))
            step(gp.tensor_tensor(rstd[:], ve[:], minus_half[:], ALU.pow))

        def gp_norm(gp, step, dst, kind, src):
            gp_scale(gp, step, mv[kind][:, 1:2])
            return gp.tensor_scalar(dst, src, mv[kind][:, 0:1], rstd[:], ALU.subtract, ALU.mult)

        def gp_stable_norm(gp, step, dst, kind, src):
            r = rinv[kind][:]
            step(gp.tensor_scalar(r2[:], mv[kind][:, 1:2], r, r, ALU.mult, ALU.mult))
            gp_scale(gp, step, r2[:])
            step(gp.tensor_tensor(rstd_r[:], rstd[:], r, ALU.mult))
            return gp.tensor_scalar(dst, src, mv[kind][:, 0:1], rstd_r[:], ALU.subtract, ALU.mult)

        def gp_take(gp, layer, s, k):
            if not static(k) or k > 0:
                hold(gp, s["xt_a"], k)
            gp.tensor_copy(cur_a[:], tile_of(k)).then_inc(s["cur_a"], 1)
            if static(k) and k == 0:
                gp.wait_ge(in_attn[layer], 16)
            hold(gp, s["cur_a"], k + 1)
            gp.tensor_tensor(tile_of(k), tile_of(k), wa(layer, "bo"), ALU.add).then_inc(s["biased"], 1)

        def gp_after_a(gp, layer, s, k):
            hold(gp, s["mv_a"], k + 1)
            if LAYERS[layer]["stable"]:
                step = steps_of(gp, s["gp_a"], k, 6)
                gp_norm(gp, step, normed[:], "a", y["a"][:]).then_inc(s["ya2"], 1)
                hold(gp, s["ya2"], k + 1)
                gp.tensor_copy(tile_of(k), normed[:])
                hold(gp, s["mv_s"], k + 1)
                if not static(k) or k > 0:
                    hold(gp, s["xt_x"], k)
                gp_stable_norm(gp, step, cur_x[:], "s", normed[:]).then_inc(s["cur_x"], 1)
            else:
                step = steps_of(gp, s["gp_a"], k, 2)
                if not static(k) or k > 0:
                    hold(gp, s["xt_x"], k)
                gp_norm(gp, step, cur_x[:], "a", y["a"][:]).then_inc(s["cur_x"], 1)
                hold(gp, s["cur_x"], k + 1)
                gp.tensor_tensor(tile_of(k), cur_x[:], wx(layer, "row"), ALU.add)

        def gp_after_x(gp, layer, s, k):
            if LAYERS[layer]["stable"]:
                step = steps_of(gp, s["gp_x"], k, 8)
                hold(gp, s["mv_z"], k + 2)
                gp_stable_norm(gp, step, z[:], "z", y["x"][:]).then_inc(s["gp_z"], 1)
                hold(gp, s["gp_z"], k + 1)
                step(gp.tensor_tensor(z[:], z[:], wx(layer, "row"), ALU.mult))
                gp.tensor_tensor(y["x"][:], z[:], tile_of(k), ALU.add).then_inc(s["y_sum"], 1)
            else:
                step = steps_of(gp, s["gp_x"], k, 3)
            hold(gp, s["mv_x"], k + (2 if LAYERS[layer]["stable"] else 1))
            step(gp_norm(gp, step, normed[:], "x", y["x"][:]))
            gp.tensor_copy(tile_of(k), normed[:]).then_inc(s["normed_x"], 1)

        def gp_layer(gp, layer):
            s = sig[layer]
            gp.wait_ge(ready_ones, 1)
            gp_take(gp, layer, s, 0)
            gp_take(gp, layer, s, 1)
            gp.wait_ge(in_cross[layer], 16)
            if layer:
                gp.wait_ge(moe["done"], BATCHES)
            gp_after_a(gp, layer, s, 0)
            gp_take(gp, layer, s, 2)
            with gp.Fori(0, LOOPS - 1) as b:
                gp_after_a(gp, layer, s, b + 1)
                gp_take(gp, layer, s, b + 3)
                gp_after_x(gp, layer, s, b)
            gp_after_a(gp, layer, s, 6)
            gp_after_x(gp, layer, s, 5)
            gp_after_a(gp, layer, s, 7)
            gp_after_x(gp, layer, s, 6)
            if layer:
                gp_ffn_take(gp, 0)
                gp_ffn_take(gp, 1)
            gp_after_x(gp, layer, s, 7)

        def gp_experts(gp):
            gp.memset(ones_b[:], 1.0).then_inc(moe["ready"], 1)
            gp.wait_ge(moe["put"], 1)
            gp.wait_ge(moe["cleared"], 16)
            for i in range(BATCHES):
                gp.indirect_dma_start(out=slots_dram[:, :], out_offset=bass.IndirectOffsetOnAxis(ap=put_at[:, i:i + 1], axis=0),
                                      in_=xres[:, i, :], in_offset=None).then_inc(moe["scattered"], 16)
            gp.wait_ge(moe["stored"], 16 * ROUNDS)
            for group, came in zip(NORM_GROUPS, gathered):
                for i in group:
                    gp.indirect_dma_start(out=back[:, i, :], out_offset=None, in_=outs_dram[:, :],
                                          in_offset=bass.IndirectOffsetOnAxis(ap=get_at[:, i:i + 1], axis=0)).then_inc(came, 16)
            for n, group in enumerate(NORM_GROUPS):
                part = slice(group[0], group[-1] + 1)
                gp.wait_ge(moe["mv"], n + 1)
                gp.tensor_scalar(ve8[:, part], mv8[:, part, 1], LN_EPS, None, ALU.add).then_inc(moe["gp"], 1)
                gp.wait_ge(moe["gp"], n + 1)
                gp.tensor_tensor(rstd8[:, part], ve8[:, part], half8[:, part], ALU.pow).then_inc(moe["rstd"], 1)
            gp.wait_ge(moe["done"], 2)

        def gp_ffn_take(gp, k):
            if not static(k) or k > 0:
                hold(gp, f["turned"], k)
            gp.tensor_copy(cur_a[:], tile_of(k)).then_inc(f["cur"], 1)

        def gp_ffn(gp):
            def routes(k):
                hold(gp, f["route"], k + 1)
                n = BANK // M2
                for c in range(2):
                    if not static(k) or k > 0:
                        hold(gp, f["flip1"] if c else f["flip0"], k)
                    hold(gp, f["hid"], k * 2 + (1 + c))
                    gp.tensor_tensor(hid_r[:, c, :].rearrange("p (e m) -> p e m", e=n), hid[:, c, :].rearrange("p (e m) -> p e m", e=n),
                                     r16["route"][:, c * n:(c + 1) * n].unsqueeze(2).to_broadcast([P, n, M2]), ALU.mult)\
                        .then_inc(f["routed"], 1)

            def norm(k):
                hold(gp, f["mv"], k + 1)
                step = steps_of(gp, f["gp"], k, 2)
                gp_scale(gp, step, mv["x"][:, 1:2])
                if not static(k) or k > 0:
                    hold(gp, f["out"], k * 16)
                gp.tensor_scalar(out_sb[:], y_f[:], mv["x"][:, 0:1], rstd[:], ALU.subtract, ALU.mult).then_inc(f["normed"], 1)

            gp.wait_ge(in_ffn, 16)
            gp_ffn_take(gp, 2)
            routes(0)
            gp_ffn_take(gp, 3)
            routes(1)
            norm(0)
            with gp.Fori(2, BATCHES - 2) as k:
                gp_ffn_take(gp, k + 2)
                routes(k)
                norm(k - 1)
            routes(BATCHES - 2)
            norm(BATCHES - 3)
            routes(BATCHES - 1)
            norm(BATCHES - 2)
            norm(BATCHES - 1)

        def sp_layer(sp, layer):
            s, keys = sig[layer], LAYERS[layer]["keys"]
            sp.wait_ge(s["k_x"], len(KEY_JOBS))
            sp.wait_ge(ready_kb, layer + 1)
            sp.dma_start(k_cur[:, :, 0:keys], k_x[:, 0, :, 0:keys]).then_inc(s["k_cur"], 16)
            with sp.Fori(1, BATCHES) as k:
                sp.wait_ge(s["scores"], k * 8 + 4)
                sp.dma_start(k_cur[:, :, 0:keys], batch_of(k_x, k)[:, :, 0:keys]).then_inc(s["k_cur"], 16)

        def sp_experts(sp):
            def weights(e, j):
                sp.dma_start(w1_sb[:, j:j + 1, :], w1[bass.ds(e, 1), :, :].rearrange("e d f -> d e f")).then_inc(w_in[j], 16)
                sp.dma_start(w2_sb[:, j, :, :], w2[bass.ds(e, 1), :, :].rearrange("e (b f) d -> f (e b) d", f=P)).then_inc(w_in[j], 16)

            for j in range(ROUND):
                weights(j, j)
            sp.wait_ge(moe["scattered"], 16 * BATCHES)
            rows = slots_dram[0:SLOTS, :].rearrange("(t p) d -> p t d", p=P)
            sp.dma_start(slot_in[:, 0:4, :], rows[:, 0:4, :]).then_inc(moe["slots_in0"], 16)
            sp.dma_start(slot_in[:, 4:, :], rows[:, 4:, :]).then_inc(moe["slots_in1"], 16)
            for j in range(ROUND):
                sp.wait_ge(moe["down"], j + 1)
                weights(ROUND + j, j)
            for i in range(ROUNDS):
                sp.wait_ge(moe["slot_out"], 2 * i + 2)
                sp.dma_start(outs_dram[i * ROUND * CAP:(i + 1) * ROUND * CAP, :].rearrange("(t p) d -> p t d", p=P), slot_out[:])\
                    .then_inc(moe["stored"], 16)

        def sp_ffn(sp):
            with sp.Fori(0, BATCHES) as k:
                sp.wait_ge(f["normed"], k + 1)
                sp.dma_start(out[bass.ds(k, 1), :, :].rearrange("b t d -> t (b d)"), out_sb[:]).then_inc(f["out"], 16)
            sp.wait_ge(f["out"], 16 * BATCHES)

        block = stack.enter_context(nc.Block())

        @block.sync
        def _(sp):
            sp.dma_start(xres[:], x.rearrange("b t d -> t b d")).then_inc(in_x, 16)
            sp.dma_start(const_sb[:], consts).then_inc(in_const, 16)
            sp.dma_start(attn_sb[0][:], attn[0]).then_inc(in_attn[0], 16)
            sp.dma_start(ctx_all[:], ctx_t.rearrange("p b c -> p (b c)")).then_inc(in_ctx, 16)
            sp.dma_start(cross_sb[0][:], cross[0]).then_inc(in_cross[0], 16)
            sp.dma_start(attn_sb[1][:], attn[1]).then_inc(in_attn[1], 16)
            sp.dma_start(cross_sb[1][:], cross[1]).then_inc(in_cross[1], 16)
            sp.dma_start(v_x[CTX:CTX + 1, :, :, 0:XD], null_v).then_inc(in_null, 16)
            sp.dma_start(ffn_sb[:], ffn).then_inc(in_ffn, 16)
            sp.wait_ge(ready_ones, 1)
            sp.dma_start(slots_dram[0:SLOTS, :].rearrange("(p n) d -> p (n d)", p=P), zeros[:]).then_inc(moe["cleared"], 16)
            sp_layer(sp, 0)
            sp_experts(sp)
            sp_layer(sp, 1)
            sp_ffn(sp)

        @block.tensor
        def _(pe):
            pe_layer(pe, 0)
            pe_experts(pe)
            pe_layer(pe, 1)
            pe_ffn(pe)

        @block.scalar
        def _(act):
            act_layer(act, 0)
            act_experts(act)
            act_layer(act, 1)
            act_ffn(act)

        @block.vector
        def _(dve):
            dve_layer(dve, 0)
            dve_experts(dve)
            dve_layer(dve, 1)
            dve_ffn(dve)

        @block.gpsimd
        def _(gp):
            gp.memset(minus_half[:], -0.5)
            gp.memset(half8[:], -0.5)
            gp.memset(zeros[:], 0.0)
            gp.memset(v_a[:, :, VD:VD + 1], 1.0)
            gp.memset(v_x[:, :, :, XD:XD + 1], 1.0).then_inc(ready_ones, 1)
            gp.wait_ge(in_x, 16)
            gp_layer(gp, 0)
            gp_experts(gp)
            gp_layer(gp, 1)
            gp_ffn(gp)


def pad_heads(w, per_head, step, blocks):
    rows = w.shape[0]
    out = np.zeros((rows, HEADS, step), w.dtype)
    out[:, :, 0:per_head] = w
    return out.reshape(rows, blocks * P)


def lay_attn0(i):
    def both(w, r):
        return np.concatenate([r.reshape(-1, HEADS, 32), w.reshape(-1, HEADS, 8)], axis=2)

    wq, wk = (pad_heads(both(i[f"L0_attn_W{n}"], i["L0_attn_Wr"]), 40, 64, 8) for n in "qk")
    bq, bk = (pad_heads(both(i[f"L0_attn_b{n}"], i["L0_attn_br"]), 40, 64, 8).reshape(8, P).T for n in "qk")
    rows = [np.broadcast_to(i[f"L0_attn_b{n}"], (P, D)) for n in "vo"]
    return np.concatenate([wq, wk, i["L0_attn_Wv"], i["L0_attn_Wo"], *rows, bq, bk], axis=1)


def lay_attn1(i):
    w = i["L1_attn_w_in"].T.reshape(D, HEADS, 3, 8)
    bias = i["L1_attn_b_in"].reshape(1, HEADS, 3, 8)
    wq, wk = (pad_heads(w[:, :, n], 8, 32, 4) for n in range(2))
    bq, bk = (pad_heads(bias[:, :, n], 8, 32, 4).reshape(4, P).T for n in range(2))
    rows = [np.broadcast_to(bias[:, :, 2].reshape(D), (P, D)), np.broadcast_to(i["L1_attn_b_out"], (P, D))]
    return np.concatenate([wq, wk, w[:, :, 2].reshape(D, D), i["L1_attn_w_out"].T, *rows, bq, bk], axis=1)


def lay_cross(wq, wk, wv, wo, row, col, null_key):
    wo = wo.reshape(8, P, D).transpose(1, 0, 2).reshape(P, 8 * D)
    return np.concatenate([wq, wk, wv, wo, np.broadcast_to(row, (P, D)), col.reshape(P, 1),
                           np.tile(null_key, 2).reshape(P, 1)], axis=1)


def lay_ffn(i):
    def wide(w):
        return w.transpose(1, 0, 2).reshape(D, E2 * M2)

    down = np.zeros((9 * P, D), np.float32)
    down[0:E2 * M2] = i["L1_ffn_w_down"].reshape(E2 * M2, D)
    down[E2 * M2:GU] = i["L1_ffn_ws_down"]
    down = down.reshape(9, P, D).transpose(1, 0, 2).reshape(P, 9 * D)
    return np.concatenate([wide(i["L1_ffn_w_gate"]), wide(i["L1_ffn_w_up"]), i["L1_ffn_ws_gate"], i["L1_ffn_ws_up"],
                           down, i["L1_ffn_gate_w"].T], axis=1)


def lay_consts(wr):
    f = np.float32
    rows = [np.broadcast_to(np.tile(np.arange(EXPERTS, 0, -1, dtype=f), BATCHES), (P, BATCHES * EXPERTS)),
            np.broadcast_to(np.arange(E2, 0, -1, dtype=f), (P, E2))]
    token = SLOTS + np.arange(BATCHES, dtype=f)[None, :] * P + np.arange(P, dtype=f)[:, None]
    return np.concatenate([np.eye(P, dtype=f), *rows, token, wr, np.triu(np.ones((P, P), f))], axis=1)


def kernel(**inputs):
    import concourse.bacc as _bacc
    from concourse.bass_utils import run_bass_kernel_spmd as _run

    i = {k: np.asarray(v) for k, v in inputs.items()}
    wkv = i["L1_xattn_Wkv"]
    arrays = {
        "x": i["x"],
        "ctx_t": i["ctx_1024"].transpose(2, 0, 1),
        "consts": lay_consts(i["L0_ffn_Wr"]),
        "attn0": lay_attn0(i),
        "attn1": lay_attn1(i),
        "cross0": lay_cross(i["L0_xattn_Wq"], i["L0_xattn_Wk"], i["L0_xattn_Wv"], i["L0_xattn_Wo"], i["L0_xattn_bo"],
                            np.ones(P, np.float32), np.zeros(XD, np.float32)),
        "cross1": lay_cross(i["L1_xattn_Wq"], wkv[:, :1024], wkv[:, 1024:], i["L1_xattn_Wo"], i["L1_xattn_g_out"],
                            i["L1_xattn_g_in"], i["L1_xattn_null_kv"][0]),
        "null_v": np.broadcast_to(i["L1_xattn_null_kv"][1], (1, BATCHES, HEADS, XD)),
        "w1": i["L0_ffn_W1"],
        "w2": i["L0_ffn_W2"],
        "ffn": lay_ffn(i),
    }
    arrays = {k: np.ascontiguousarray(v) for k, v in arrays.items()}
    nc = _bacc.Bacc("TRN2", target_bir_lowering=False, num_devices=1)
    a = {n: nc.dram_tensor(n, v.shape, mybir.dt.from_np(v.dtype), kind="ExternalInput").ap() for n, v in arrays.items()}
    out = nc.dram_tensor("out", (BATCHES, TOKENS, D), F32, kind="ExternalOutput").ap()
    decoder(nc, a["x"], a["ctx_t"], a["consts"], (a["attn0"], a["attn1"]), (a["cross0"], a["cross1"]), a["null_v"],
            a["w1"], a["w2"], a["ffn"], out)
    r = _run(nc, [arrays], core_ids=[0])
    return r.results[0]["out"]
```
